# Optimizing a Trainium2 kernel written in Bass

```python
import numpy as np
import jax
import jax.numpy as jnp

def _softmax(x, axis=-1):
    return jax.nn.softmax(x, axis=axis)

def _gelu(x):
    return jax.nn.gelu(x, approximate=True)

def _silu(x):
    return jax.nn.silu(x)

def _sigmoid(x):
    return jax.nn.sigmoid(x)

def _layernorm(x, axis=-1, eps=1e-05):
    m = jnp.mean(x, axis=axis, keepdims=True)
    v = jnp.var(x, axis=axis, keepdims=True)
    return (x - m) / jnp.sqrt(v + eps)

def _scatter_add(tgt, idx, src, axis=0):
    return tgt.at[idx].add(src)

def _segment_sum(src, seg, n):
    return jax.ops.segment_sum(src, seg, n)
kernel_name = 'mk_dlrm_tower_d1_rec_r8_620509'

def setup_inputs(seed: int=0):
    np.random.seed(seed)
    _w = jnp.asarray

    def _rec_inputs():
        import jax
        import jax.numpy as jnp
        _tk = jax.random.key(seed)
        dense_ctx = jax.random.normal(jax.random.fold_in(_tk, 190), (1024, 16), jnp.float32)
        ids = jnp.stack([jax.random.randint(jax.random.fold_in(_tk, 200 + f), (1024,), 0, v, jnp.int32) for f, v in enumerate([12500, 125000, 1250, 12500, 12500, 125000, 12500, 1250, 1000, 12500, 125000, 1250, 12500, 1250, 125000, 1000, 12500, 1250, 1000, 1000, 1250, 1000, 1250, 1000, 125000, 125000, 1000, 125000, 125000, 12500, 1250, 12500, 1000, 1000, 12500, 1250, 125000, 1250, 1000])], axis=1)
        tbl_0 = 0.05 * jax.random.normal(jax.random.fold_in(_tk, 500 + 0), (12500, 16), jnp.float32)
        tbl_1 = 0.05 * jax.random.normal(jax.random.fold_in(_tk, 500 + 1), (125000, 16), jnp.float32)
        tbl_2 = 0.05 * jax.random.normal(jax.random.fold_in(_tk, 500 + 2), (1250, 16), jnp.float32)
        tbl_3 = 0.05 * jax.random.normal(jax.random.fold_in(_tk, 500 + 3), (12500, 16), jnp.float32)
        tbl_4 = 0.05 * jax.random.normal(jax.random.fold_in(_tk, 500 + 4), (12500, 16), jnp.float32)
        tbl_5 = 0.05 * jax.random.normal(jax.random.fold_in(_tk, 500 + 5), (125000, 16), jnp.float32)
        tbl_6 = 0.05 * jax.random.normal(jax.random.fold_in(_tk, 500 + 6), (12500, 16), jnp.float32)
        tbl_7 = 0.05 * jax.random.normal(jax.random.fold_in(_tk, 500 + 7), (1250, 16), jnp.float32)
        tbl_8 = 0.05 * jax.random.normal(jax.random.fold_in(_tk, 500 + 8), (1000, 16), jnp.float32)
        tbl_9 = 0.05 * jax.random.normal(jax.random.fold_in(_tk, 500 + 9), (12500, 16), jnp.float32)
        tbl_10 = 0.05 * jax.random.normal(jax.random.fold_in(_tk, 500 + 10), (125000, 16), jnp.float32)
        tbl_11 = 0.05 * jax.random.normal(jax.random.fold_in(_tk, 500 + 11), (1250, 16), jnp.float32)
        tbl_12 = 0.05 * jax.random.normal(jax.random.fold_in(_tk, 500 + 12), (12500, 16), jnp.float32)
        tbl_13 = 0.05 * jax.random.normal(jax.random.fold_in(_tk, 500 + 13), (1250, 16), jnp.float32)
        tbl_14 = 0.05 * jax.random.normal(jax.random.fold_in(_tk, 500 + 14), (125000, 16), jnp.float32)
        tbl_15 = 0.05 * jax.random.normal(jax.random.fold_in(_tk, 500 + 15), (1000, 16), jnp.float32)
        tbl_16 = 0.05 * jax.random.normal(jax.random.fold_in(_tk, 500 + 16), (12500, 16), jnp.float32)
        tbl_17 = 0.05 * jax.random.normal(jax.random.fold_in(_tk, 500 + 17), (1250, 16), jnp.float32)
        tbl_18 = 0.05 * jax.random.normal(jax.random.fold_in(_tk, 500 + 18), (1000, 16), jnp.float32)
        tbl_19 = 0.05 * jax.random.normal(jax.random.fold_in(_tk, 500 + 19), (1000, 16), jnp.float32)
        tbl_20 = 0.05 * jax.random.normal(jax.random.fold_in(_tk, 500 + 20), (1250, 16), jnp.float32)
        tbl_21 = 0.05 * jax.random.normal(jax.random.fold_in(_tk, 500 + 21), (1000, 16), jnp.float32)
        tbl_22 = 0.05 * jax.random.normal(jax.random.fold_in(_tk, 500 + 22), (1250, 16), jnp.float32)
        tbl_23 = 0.05 * jax.random.normal(jax.random.fold_in(_tk, 500 + 23), (1000, 16), jnp.float32)
        tbl_24 = 0.05 * jax.random.normal(jax.random.fold_in(_tk, 500 + 24), (125000, 16), jnp.float32)
        tbl_25 = 0.05 * jax.random.normal(jax.random.fold_in(_tk, 500 + 25), (125000, 16), jnp.float32)
        tbl_26 = 0.05 * jax.random.normal(jax.random.fold_in(_tk, 500 + 26), (1000, 16), jnp.float32)
        tbl_27 = 0.05 * jax.random.normal(jax.random.fold_in(_tk, 500 + 27), (125000, 16), jnp.float32)
        tbl_28 = 0.05 * jax.random.normal(jax.random.fold_in(_tk, 500 + 28), (125000, 16), jnp.float32)
        tbl_29 = 0.05 * jax.random.normal(jax.random.fold_in(_tk, 500 + 29), (12500, 16), jnp.float32)
        tbl_30 = 0.05 * jax.random.normal(jax.random.fold_in(_tk, 500 + 30), (1250, 16), jnp.float32)
        tbl_31 = 0.05 * jax.random.normal(jax.random.fold_in(_tk, 500 + 31), (12500, 16), jnp.float32)
        tbl_32 = 0.05 * jax.random.normal(jax.random.fold_in(_tk, 500 + 32), (1000, 16), jnp.float32)
        tbl_33 = 0.05 * jax.random.normal(jax.random.fold_in(_tk, 500 + 33), (1000, 16), jnp.float32)
        tbl_34 = 0.05 * jax.random.normal(jax.random.fold_in(_tk, 500 + 34), (12500, 16), jnp.float32)
        tbl_35 = 0.05 * jax.random.normal(jax.random.fold_in(_tk, 500 + 35), (1250, 16), jnp.float32)
        tbl_36 = 0.05 * jax.random.normal(jax.random.fold_in(_tk, 500 + 36), (125000, 16), jnp.float32)
        tbl_37 = 0.05 * jax.random.normal(jax.random.fold_in(_tk, 500 + 37), (1250, 16), jnp.float32)
        tbl_38 = 0.05 * jax.random.normal(jax.random.fold_in(_tk, 500 + 38), (1000, 16), jnp.float32)
        _rk = jax.random.fold_in(_tk, 7)
        W_top1 = 0.0606339 * jax.random.normal(jax.random.fold_in(_tk, 801), (272, 512), jnp.float32)
        W_top2 = 0.0441942 * jax.random.normal(jax.random.fold_in(_tk, 802), (512, 256), jnp.float32)
        W_top3 = 0.0625 * jax.random.normal(jax.random.fold_in(_tk, 803), (256, 1), jnp.float32)
        b_top1 = jnp.zeros((512,), jnp.float32)
        b_top2 = jnp.zeros((256,), jnp.float32)
        return (dense_ctx, ids, tbl_0, tbl_1, tbl_2, tbl_3, tbl_4, tbl_5, tbl_6, tbl_7, tbl_8, tbl_9, tbl_10, tbl_11, tbl_12, tbl_13, tbl_14, tbl_15, tbl_16, tbl_17, tbl_18, tbl_19, tbl_20, tbl_21, tbl_22, tbl_23, tbl_24, tbl_25, tbl_26, tbl_27, tbl_28, tbl_29, tbl_30, tbl_31, tbl_32, tbl_33, tbl_34, tbl_35, tbl_36, tbl_37, tbl_38, W_top1, b_top1, W_top2, b_top2, W_top3)
    dense_ctx, ids, tbl_0, tbl_1, tbl_2, tbl_3, tbl_4, tbl_5, tbl_6, tbl_7, tbl_8, tbl_9, tbl_10, tbl_11, tbl_12, tbl_13, tbl_14, tbl_15, tbl_16, tbl_17, tbl_18, tbl_19, tbl_20, tbl_21, tbl_22, tbl_23, tbl_24, tbl_25, tbl_26, tbl_27, tbl_28, tbl_29, tbl_30, tbl_31, tbl_32, tbl_33, tbl_34, tbl_35, tbl_36, tbl_37, tbl_38, W_top1, b_top1, W_top2, b_top2, W_top3 = _rec_inputs()

    def _L0_rec_setup():
        import jax, jax.numpy as jnp
        import numpy as np
        B, M0, D = (256, 39, 16)
        CIN_SIZE = [128, 128]

        def _cin(inputs, weights):
            X0 = inputs
            Xi = inputs
            res = []
            for W in weights:
                mi = Xi.shape[1]
                z = jnp.einsum('bmd,bnd->bdmn', X0, Xi)
                z = z.reshape(z.shape[0], z.shape[1], M0 * mi)
                Xi = jnp.einsum('bdp,po->bod', z, W)
                res.append(Xi)
            res = jnp.concatenate(res, axis=1)
            return jnp.sum(res, axis=-1)
        key = jax.random.key(seed)
        k1, k2, k3 = jax.random.split(key, 3)
        inputs = jax.random.normal(k1, (B, M0, D), dtype=jnp.float32)
        W0 = jax.random.normal(k2, (M0 * M0, CIN_SIZE[0]), dtype=jnp.float32) * 0.05
        W1 = jax.random.normal(k3, (M0 * CIN_SIZE[0], CIN_SIZE[1]), dtype=jnp.float32) * 0.05
        return {'inputs': inputs, 'W0': W0, 'W1': W1}
    _L0_rec_all = _L0_rec_setup()
    _L0_rec_in = {k: v for k, v in _L0_rec_all.items() if k in ('W0', 'W1')}
    del _L0_rec_all
    return {'dense_ctx': dense_ctx, 'ids': ids, 'tbl_0': tbl_0, 'tbl_1': tbl_1, 'tbl_2': tbl_2, 'tbl_3': tbl_3, 'tbl_4': tbl_4, 'tbl_5': tbl_5, 'tbl_6': tbl_6, 'tbl_7': tbl_7, 'tbl_8': tbl_8, 'tbl_9': tbl_9, 'tbl_10': tbl_10, 'tbl_11': tbl_11, 'tbl_12': tbl_12, 'tbl_13': tbl_13, 'tbl_14': tbl_14, 'tbl_15': tbl_15, 'tbl_16': tbl_16, 'tbl_17': tbl_17, 'tbl_18': tbl_18, 'tbl_19': tbl_19, 'tbl_20': tbl_20, 'tbl_21': tbl_21, 'tbl_22': tbl_22, 'tbl_23': tbl_23, 'tbl_24': tbl_24, 'tbl_25': tbl_25, 'tbl_26': tbl_26, 'tbl_27': tbl_27, 'tbl_28': tbl_28, 'tbl_29': tbl_29, 'tbl_30': tbl_30, 'tbl_31': tbl_31, 'tbl_32': tbl_32, 'tbl_33': tbl_33, 'tbl_34': tbl_34, 'tbl_35': tbl_35, 'tbl_36': tbl_36, 'tbl_37': tbl_37, 'tbl_38': tbl_38, 'W_top1': W_top1, 'b_top1': b_top1, 'W_top2': W_top2, 'b_top2': b_top2, 'W_top3': W_top3, 'L0_rec_W0': _L0_rec_in['W0'], 'L0_rec_W1': _L0_rec_in['W1']}

def reference(dense_ctx, ids, tbl_0, tbl_1, tbl_2, tbl_3, tbl_4, tbl_5, tbl_6, tbl_7, tbl_8, tbl_9, tbl_10, tbl_11, tbl_12, tbl_13, tbl_14, tbl_15, tbl_16, tbl_17, tbl_18, tbl_19, tbl_20, tbl_21, tbl_22, tbl_23, tbl_24, tbl_25, tbl_26, tbl_27, tbl_28, tbl_29, tbl_30, tbl_31, tbl_32, tbl_33, tbl_34, tbl_35, tbl_36, tbl_37, tbl_38, W_top1, b_top1, W_top2, b_top2, W_top3, L0_rec_W0, L0_rec_W1):
    import jax
    import jax.numpy as jnp

    def _L0_rec_ref(inputs, W0, W1):
        import jax, jax.numpy as jnp
        import numpy as np
        B, M0, D = (256, 39, 16)
        CIN_SIZE = [128, 128]

        def _cin(inputs, weights):
            X0 = inputs
            Xi = inputs
            res = []
            for W in weights:
                mi = Xi.shape[1]
                z = jnp.einsum('bmd,bnd->bdmn', X0, Xi)
                z = z.reshape(z.shape[0], z.shape[1], M0 * mi)
                Xi = jnp.einsum('bdp,po->bod', z, W)
                res.append(Xi)
            res = jnp.concatenate(res, axis=1)
            return jnp.sum(res, axis=-1)
        return _cin(inputs, [W0, W1])
    e = jnp.stack([tbl_0[ids[:, 0]], tbl_1[ids[:, 1]], tbl_2[ids[:, 2]], tbl_3[ids[:, 3]], tbl_4[ids[:, 4]], tbl_5[ids[:, 5]], tbl_6[ids[:, 6]], tbl_7[ids[:, 7]], tbl_8[ids[:, 8]], tbl_9[ids[:, 9]], tbl_10[ids[:, 10]], tbl_11[ids[:, 11]], tbl_12[ids[:, 12]], tbl_13[ids[:, 13]], tbl_14[ids[:, 14]], tbl_15[ids[:, 15]], tbl_16[ids[:, 16]], tbl_17[ids[:, 17]], tbl_18[ids[:, 18]], tbl_19[ids[:, 19]], tbl_20[ids[:, 20]], tbl_21[ids[:, 21]], tbl_22[ids[:, 22]], tbl_23[ids[:, 23]], tbl_24[ids[:, 24]], tbl_25[ids[:, 25]], tbl_26[ids[:, 26]], tbl_27[ids[:, 27]], tbl_28[ids[:, 28]], tbl_29[ids[:, 29]], tbl_30[ids[:, 30]], tbl_31[ids[:, 31]], tbl_32[ids[:, 32]], tbl_33[ids[:, 33]], tbl_34[ids[:, 34]], tbl_35[ids[:, 35]], tbl_36[ids[:, 36]], tbl_37[ids[:, 37]], tbl_38[ids[:, 38]]], axis=1)
    z = _L0_rec_ref(e, L0_rec_W0, L0_rec_W1)
    z = z.reshape(z.shape[0], -1)
    h = jnp.concatenate([z, dense_ctx], axis=1)
    h = jnp.maximum(h @ W_top1 + b_top1, 0.0)
    h = jnp.maximum(h @ W_top2 + b_top2, 0.0)
    y = h @ W_top3
    return y

_drawn_inputs = setup_inputs


def setup_inputs(seed=0):
    import zlib

    import numpy as np

    out = dict(_drawn_inputs(seed))
    spreads = {'b_top1': (0.0, 0.1), 'b_top2': (0.0, 0.1)}
    factors = {'tbl_0': 4.915,
     'tbl_1': 5.15,
     'tbl_2': 4.834,
     'tbl_3': 5.156,
     'tbl_4': 5.491,
     'tbl_5': 5.366,
     'tbl_6': 5.031,
     'tbl_7': 4.947,
     'tbl_8': 4.941,
     'tbl_9': 4.655,
     'tbl_10': 5.261,
     'tbl_11': 4.943,
     'tbl_12': 4.685,
     'tbl_13': 4.651,
     'tbl_14': 4.715,
     'tbl_15': 5.126,
     'tbl_16': 5.45,
     'tbl_17': 5.003,
     'tbl_18': 4.978,
     'tbl_19': 5.144,
     'tbl_20': 4.881,
     'tbl_21': 5.242,
     'tbl_22': 4.772,
     'tbl_23': 4.852,
     'tbl_24': 4.726,
     'tbl_25': 4.633,
     'tbl_26': 5.018,
     'tbl_27': 5.221,
     'tbl_28': 4.969,
     'tbl_29': 4.911,
     'tbl_30': 5.428,
     'tbl_31': 4.519,
     'tbl_32': 5.073,
     'tbl_33': 4.808,
     'tbl_34': 4.663,
     'tbl_35': 4.984,
     'tbl_36': 4.759,
     'tbl_37': 4.842,
     'tbl_38': 5.011,
     'L0_rec_W1': 5.468}
    for name, (base, spread) in spreads.items():
        noise = np.random.default_rng([zlib.crc32(name.encode()), seed]).standard_normal(out[name].shape)
        drawn = base * np.exp(spread * noise) if base else spread * noise
        out[name] = jnp.asarray(drawn.astype(out[name].dtype))
    for name, factor in factors.items():
        out[name] = (out[name] * factor).astype(out[name].dtype)
    return out
```

```python
from contextlib import ExitStack

import numpy as np

import concourse.bass as bass
from concourse import mybir

F32 = mybir.dt.float32
BF16 = mybir.dt.bfloat16
I32 = mybir.dt.int32
U32 = mybir.dt.uint32
ALU = mybir.AluOpType
ACT = mybir.ActivationFunctionType

P = 128
BATCH = 1024
NF = 39
D = 16
NO = 128
ND = 16
H1, H2 = 512, 256

TILE = P
TILES = BATCH // TILE
STEP = 32
COLS = STEP * D
SPT = TILE // STEP
STEPS = BATCH // STEP
PAIR = 2 * TILE
PAIRS = BATCH // PAIR
SPP = PAIR // STEP
GROUPS = COLS // P
STRIPS = 2
OWNERS = 4

SHIFTS = NF // 2 + 1
ROWS = 3 * NF
CHUNKS = -(-SHIFTS // 3)
KROWS = [min(SHIFTS - 3 * c, 3) * NF for c in range(CHUNKS)]
NM = NF + 1
ZBUFS = 4
LAG = 2


def constants():
    select = np.zeros((3, NF, 1 + CHUNKS, ROWS), np.float32)
    for row in range(ROWS):
        m, j = row % NF, row // NF
        select[:, m, 0, row] = 1
        for c in range(CHUNKS):
            if row < KROWS[c]:
                select[:, (m + 3 * c + j) % NF, 1 + c, row] = 1
    stack = np.zeros((3, NF, NF), np.float32)
    stack[:, range(NF), range(NF)] = 1
    own = np.zeros((STRIPS, OWNERS, D, OWNERS), np.float32)
    own[:, range(OWNERS), :, range(OWNERS)] = 1
    return (select.reshape(ROWS, 1 + CHUNKS, ROWS), stack.reshape(ROWS, NF),
            own.reshape(P, OWNERS), np.eye(P, dtype=np.float32))


def build(nc, ids, tables, dense, w0a, w0b, w1, wt1, wt1d, wt2, wt3, b1, b2,
          select_d, stack_d, own_d, eye_d, out):
    with ExitStack() as ctx:
        def sb(name, shape, dt=F32):
            return ctx.enter_context(nc.sbuf_tensor(name, shape, dt))

        def bank(name, *shape):
            return ctx.enter_context(nc.psum_tensor(name, [P, *shape], F32))

        def sem(name):
            return ctx.enter_context(nc.semaphore(name))

        idx = sb("idx", [P, 2, NF], I32)
        select = sb("select", [P, 1 + CHUNKS, ROWS], BF16)
        stack = sb("stack", [P, NF], BF16)
        own = sb("own", [P, OWNERS])
        eye = sb("eye", [P, P])
        eye_bf = sb("eye_bf", [P, P], BF16)
        select_f = sb("select_f", [P, 1 + CHUNKS, ROWS])
        stack_f = sb("stack_f", [P, NF])
        ws_a = sb("ws_a", [P, CHUNKS, NO])
        ws_b = sb("ws_b", [P, CHUNKS, NO])
        ws = sb("ws", [P, CHUNKS, NO])
        w1_sb = sb("w1_sb", [P, NF, NO])
        wt1_sb = sb("wt1_sb", [P, 2, H1])
        wt1d_sb = sb("wt1d_sb", [P, H1])
        wt2_sb = sb("wt2_sb", [P, H1 // P, H2])
        wt3_sb = sb("wt3_sb", [P, H2 // P])
        b1_sb = sb("b1_sb", [P, H1 // P])
        b2_sb = sb("b2_sb", [P, H2 // P])
        dense_sb = sb("dense_sb", [P, PAIR])

        emb = sb("emb", [P, 2, NF, D])
        rest = sb("rest", [P, NF, D])
        parts = sb("parts", [P, D, 3, NF], BF16)
        x3 = sb("x3", [P, 2, TILE, D], BF16)
        first = sb("first", [P, 2, COLS])
        z = sb("z", [P, ZBUFS, COLS])
        xb = sb("xb", [P, 4, GROUPS, OWNERS, NM])
        x1 = sb("x1", [P, 2, COLS])
        x1t = sb("x1t", [P, 2, GROUPS, NO])
        prod = sb("prod", [P, NM, PAIR])
        out2 = sb("out2", [P, PAIR])
        h1 = sb("h1", [P, H1 // P, PAIR])
        h2 = sb("h2", [P, H2 // P, PAIR])
        y = sb("y", [1, PAIR])

        second_ps = [bank(f"second_ps{i}", COLS) for i in range(2)]
        work_ps = bank("work_ps", COLS)
        x1_ps = bank("x1_ps", COLS)
        prod_ps = bank("prod_ps", 2 * STRIPS, 512)

        idx_loaded = [sem(f"idx_loaded{i}") for i in range(2)]
        consts_loaded = sem("consts_loaded")
        ws_loaded = sem("ws_loaded")
        late_loaded = sem("late_loaded")
        dense_loaded = sem("dense_loaded")
        gathered = [sem(f"gathered{i}") for i in range(2)]
        consts_ready = sem("consts_ready")
        ws_ready = sem("ws_ready")
        hi_ready = sem("hi_ready")
        rest_ready = sem("rest_ready")
        mid_ready = sem("mid_ready")
        parts_ready = sem("parts_ready")
        parts_turned = sem("parts_turned")
        x3_ready = sem("x3_ready")
        first_picked = sem("first_picked")
        first_ready = sem("first_ready")
        second_picked = sem("second_picked")
        z_ready = sem("z_ready")
        z_used = sem("z_used")
        x_turned = sem("x_turned")
        xb_ready = sem("xb_ready")
        x1_ready = sem("x1_ready")
        x1_turned = sem("x1_turned")
        x1t_ready = sem("x1t_ready")
        prod_done = sem("prod_done")
        prod_ready = sem("prod_ready")
        out2_done = sem("out2_done")
        out2_ready = sem("out2_ready")
        h1_done = sem("h1_done")
        h1_ready = sem("h1_ready")
        h2_done = sem("h2_done")
        h2_ready = sem("h2_ready")
        y_done = sem("y_done")
        y_ready = sem("y_ready")
        y_stored = sem("y_stored")

        CONSTS = 4
        LATE = 7

        def has(s, low=0):
            return not isinstance(s, int) or low <= s < STEPS

        def opens_tile(s, j):
            return j % SPT == SPT - 1 and has(s + 1)

        block = ctx.enter_context(nc.Block())

        @block.sync
        def _(sp):
            def load_idx(t, parity):
                sp.dma_start(idx[:, parity, :], ids[:, bass.ds(t * NF, NF)]).then_inc(idx_loaded[parity], 16)

            load_idx(0, 0)
            load_idx(1, 1)
            sp.dma_start(eye[:, :], eye_d).then_inc(consts_loaded, 16)
            sp.dma_start(select_f[0:ROWS, :, :], select_d).then_inc(consts_loaded, 16)
            sp.dma_start(stack_f[0:ROWS, :], stack_d).then_inc(consts_loaded, 16)
            sp.dma_start(own[:, :], own_d).then_inc(consts_loaded, 16)
            sp.dma_start(ws_a[0:ROWS, :, :], w0a).then_inc(ws_loaded, 16)
            sp.dma_start(ws_b[0:ROWS, :, :], w0b).then_inc(ws_loaded, 16)
            sp.dma_start(w1_sb[:, :, :], w1.rearrange("(m n) o -> n m o", n=NO)).then_inc(late_loaded, 16)
            sp.dma_start(wt1_sb[:, :, :], wt1.rearrange("(c p) h -> p c h", p=P)).then_inc(late_loaded, 16)
            sp.dma_start(wt1d_sb[0:ND, :], wt1d).then_inc(late_loaded, 16)
            sp.dma_start(wt2_sb[:, :, :], wt2.rearrange("(c p) h -> p c h", p=P)).then_inc(late_loaded, 16)
            sp.dma_start(wt3_sb[:, :], wt3).then_inc(late_loaded, 16)
            sp.dma_start(b1_sb[:, :], b1).then_inc(late_loaded, 16)
            sp.dma_start(b2_sb[:, :], b2).then_inc(late_loaded, 16)

            def load_dense(k):
                sp.dma_start(dense_sb[0:ND, :], dense[:, bass.ds(k * PAIR, PAIR)]).then_inc(dense_loaded, 16)

            def store(k):
                sp.wait_ge(y_ready, k + 2)
                sp.dma_start(out[bass.ds(k * PAIR, PAIR), :].rearrange("b a -> a b"),
                             y[0:1, :]).then_inc(y_stored, 16)

            load_dense(0)
            with sp.Fori(0, PAIRS - 1) as k:
                for parity in range(2):
                    sp.wait_ge(gathered[parity], 16 * NF * (k + 1))
                    load_idx(2 * k + 2 + parity, parity)
                store(k)
                sp.wait_ge(y_stored, 16 * (k + 1))
                load_dense(k + 1)
            store(PAIRS - 1)
            sp.wait_ge(y_stored, 16 * PAIRS)

        @block.gpsimd
        def _(pool):
            def gather(k, parity):
                pool.wait_ge(idx_loaded[parity], 16 * k + 16)
                pool.nop(nofuse=True)
                for f in range(NF):
                    pool.indirect_dma_start(
                        emb[:, parity, f, :], None, tables[f],
                        bass.IndirectOffsetOnAxis(ap=idx[:, parity, f:f + 1].bitcast(U32), axis=0),
                    ).then_inc(gathered[parity], 16)

            gather(0, 0)
            gather(0, 1)
            with pool.Fori(1, PAIRS) as k:
                for parity in range(2):
                    pool.wait_ge(rest_ready, 2 * k + parity - 1)
                    gather(k, parity)

        @block.tensor
        def _(pe):
            def columns(j):
                u = j % SPP
                v = x3[0:ROWS, u // SPT, (u % SPT) * STEP:(u % SPT + 1) * STEP, :]
                return v.rearrange("p b d -> p (b d)")

            def turn_parts(t, half):
                if half == 0:
                    pe.wait_ge(parts_ready, t + 1)
                dst = work_ps[:, :].bitcast(BF16)
                for i in range(8):
                    last = nc.tensor.transpose(dst[0:ROWS, i * P:(i + 1) * P],
                                               parts[:, 8 * half + i, :, :].rearrange("p a m -> p (a m)"),
                                               eye_bf[:, :])
                last.then_inc(parts_turned, 1)

            def pick_first(j):
                nc.tensor.matmul(work_ps[0:ROWS, :], select[0:ROWS, 0, :], columns(j),
                                 start=True, stop=True).then_inc(first_picked, 1)

            def pick_second(s, j, c):
                n = CHUNKS * s + c
                if not isinstance(n, int) or n >= 2:
                    pe.wait_ge(z_ready, n - 1)
                nc.tensor.matmul(second_ps[(CHUNKS * j + c) % 2][0:KROWS[c], :],
                                 select[0:ROWS, 1 + c, 0:KROWS[c]], columns(j),
                                 start=True, stop=True).then_inc(second_picked, 1)

            def layer1(s, j, c):
                pe.wait_ge(z_ready, CHUNKS * s + c + 1)
                if c == 0 and has(s, 1):
                    pe.wait_ge(x1_ready, s)
                nc.tensor.matmul(x1_ps[:, :], ws[0:KROWS[c], c, :],
                                 z[0:KROWS[c], (CHUNKS * j + c) % ZBUFS, :],
                                 start=(c == 0), stop=(c == CHUNKS - 1)).then_inc(z_used, 1)

            def turn_x1(s, j):
                pe.wait_ge(x1_ready, s + 1)
                for g in range(GROUPS):
                    last = nc.tensor.transpose(work_ps[:, g * P:(g + 1) * P],
                                               x1[:, j % 2, g * P:(g + 1) * P], eye[:, :])
                last.then_inc(x1_turned, 1)

            def turn_x(j):
                for g in range(GROUPS):
                    last = nc.tensor.matmul(work_ps[:, g * NF:(g + 1) * NF], columns(j)[:, g * P:(g + 1) * P],
                                            stack[0:ROWS, :], start=True, stop=True)
                last.then_inc(x_turned, 1)

            def multiply_layers(s, j):
                pe.wait_ge(x1t_ready, s + 1)
                pe.wait_ge(xb_ready, s + 1)
                if has(s, 1):
                    pe.wait_ge(prod_ready, s)
                for g in range(GROUPS):
                    for q in range(STRIPS):
                        r = slice(64 * q, 64 * q + 64)
                        at = (g % 2) * OWNERS * NM
                        last = nc.tensor.matmul(prod_ps[:, 2 * q + g // 2, at:at + OWNERS * NM],
                                                x1t[r, j % 2, g, :],
                                                xb[r, j % 4, g, :, :].rearrange("p b m -> p (b m)"),
                                                start=True, stop=True)
                last.then_inc(prod_done, 1)

            def step(k, j):
                s = SPP * k + j
                tile = 2 * k + j // SPT
                for c in range(CHUNKS):
                    if c + 1 < CHUNKS:
                        pick_second(s, j, c + 1)
                    elif has(s + 1):
                        if opens_tile(s, j):
                            pe.wait_ge(x3_ready, 2 * tile + 4)
                        pick_second(s + 1, j + 1, 0)
                    if c == 0 and has(s, LAG):
                        if j == LAG:
                            pe.wait_ge(y_ready, k + 1)
                        multiply_layers(s - LAG, j - LAG)
                    layer1(s, j, c)
                    if c == 0 and has(s, 1):
                        pe.wait_ge(first_ready, s + 1)
                        turn_x1(s - 1, j - 1)
                    if c == 1:
                        if has(s, 1):
                            pe.wait_ge(x1t_ready, s)
                        else:
                            pe.wait_ge(first_ready, s + 1)
                        turn_x(j)
                    if c == 3 and opens_tile(s, j):
                        pe.wait_ge(xb_ready, s + 1)
                        turn_parts(tile + 1, 0)
                    if c == 4 and opens_tile(s, j):
                        pe.wait_ge(x3_ready, 2 * tile + 3)
                        turn_parts(tile + 1, 1)
                    if c == 5 and has(s + 1):
                        if opens_tile(s, j):
                            pe.wait_ge(x3_ready, 2 * tile + 4)
                        else:
                            pe.wait_ge(xb_ready, s + 1)
                        pick_first(j + 1)

            def layer2(k):
                pe.wait_ge(prod_ready, SPP * k + SPP)
                for m in range(NF):
                    last = nc.tensor.matmul(prod_ps[:, 0, 0:PAIR], w1_sb[:, m, :], prod[:, m, :],
                                            start=(m == 0), stop=(m == NF - 1))
                last.then_inc(out2_done, 1)

            def mlp(k):
                pe.wait_ge(dense_loaded, 16 * k + 16)
                for i in range(H1 // P):
                    o = prod_ps[:, 1 + i // 2, (i % 2) * PAIR:(i % 2 + 1) * PAIR]
                    cols = slice(i * P, (i + 1) * P)
                    nc.tensor.matmul(o, wt1_sb[:, 0, cols], prod[:, NF, :], start=True, stop=False)
                    nc.tensor.matmul(o, wt1d_sb[0:ND, cols], dense_sb[0:ND, :], start=False, stop=False)
                    if i == 0:
                        pe.wait_ge(out2_ready, k + 1)
                    last = nc.tensor.matmul(o, wt1_sb[:, 1, cols], out2[:, :], start=False, stop=True)
                last.then_inc(h1_done, 1)
                pe.wait_ge(h1_ready, k + 1)
                for j in range(H2 // P):
                    for i in range(H1 // P):
                        last = nc.tensor.matmul(prod_ps[:, 3, j * PAIR:(j + 1) * PAIR],
                                                wt2_sb[:, i, j * P:(j + 1) * P], h1[:, i, :],
                                                start=(i == 0), stop=(i == H1 // P - 1))
                last.then_inc(h2_done, 1)
                pe.wait_ge(h2_ready, k + 1)
                for j in range(H2 // P):
                    last = nc.tensor.matmul(prod_ps[0:1, 0, 0:PAIR], wt3_sb[:, j:j + 1], h2[:, j, :],
                                            start=(j == 0), stop=(j == H2 // P - 1))
                last.then_inc(y_done, 1)

            pe.wait_ge(consts_ready, 1)
            turn_parts(0, 0)
            pe.wait_ge(x3_ready, 1)
            turn_parts(0, 1)
            pe.wait_ge(x3_ready, 2)
            pick_first(0)
            pick_second(0, 0, 0)
            pe.wait_ge(ws_ready, 1)
            for j in range(LAG):
                step(0, j)
            pe.wait_ge(late_loaded, 16 * LATE)
            with pe.Fori(0, PAIRS - 1) as k:
                for j in range(LAG, LAG + SPP):
                    step(k, j)
                layer2(k)
                mlp(k)
            for j in range(LAG, SPP):
                step(PAIRS - 1, j)
            end = STEPS - 1
            multiply_layers(end - 1, SPP - 2)
            turn_x1(end, SPP - 1)
            multiply_layers(end, SPP - 1)
            layer2(PAIRS - 1)
            mlp(PAIRS - 1)

        @block.scalar
        def _(act):
            def copy_parts(t, parity, half):
                act.wait_ge(parts_turned, 2 * t + half + 1)
                nc.scalar.copy(x3[0:ROWS, parity, :, 8 * half:8 * half + 8].rearrange("p b d -> p d b"),
                               work_ps[0:ROWS, :].bitcast(BF16).rearrange("p (d b) -> p d b", d=8)
                               ).then_inc(x3_ready, 1)

            def copy_first(s, j):
                act.wait_ge(first_picked, s + 1)
                nc.scalar.copy(first[0:ROWS, j % 2, :], work_ps[0:ROWS, :]).then_inc(first_ready, 1)

            def copy_x1(s, j):
                act.wait_ge(z_used, CHUNKS * s + CHUNKS)
                nc.scalar.copy(x1[:, j % 2, :], x1_ps[:, :]).then_inc(x1_ready, 1)

            def copy_prod(s, j):
                act.wait_ge(prod_done, s + 1)
                b = (j % SPP) * STEP
                nc.scalar.copy(prod[:, :, b:b + STEP].rearrange("p m (q b) -> p q b m", q=2 * STRIPS),
                               prod_ps[:, :, 0:2 * OWNERS * NM].rearrange("p q (b m) -> p q b m", m=NM)
                               ).then_inc(prod_ready, 1)

            def copy_x1t(s, j):
                act.wait_ge(x1_turned, s + 1)
                nc.scalar.copy(x1t[:, j % 2, :, :].rearrange("p g n -> p (g n)"),
                               work_ps[:, :]).then_inc(x1t_ready, 1)

            def step(k, j):
                s = SPP * k + j
                tile = 2 * k + j // SPT
                if has(s, 1):
                    copy_x1(s - 1, j - 1)
                if has(s, LAG):
                    copy_prod(s - LAG, j - LAG)
                if has(s, 1):
                    copy_x1t(s - 1, j - 1)
                if opens_tile(s, j):
                    copy_parts(tile + 1, (j // SPT + 1) % 2, 0)
                    copy_parts(tile + 1, (j // SPT + 1) % 2, 1)
                if has(s + 1):
                    copy_first(s + 1, j + 1)

            copy_parts(0, 0, 0)
            copy_parts(0, 0, 1)
            copy_first(0, 0)
            for j in range(LAG):
                step(0, j)
            with act.Fori(0, PAIRS - 1) as k:
                for j in range(LAG, LAG + SPP):
                    step(k, j)
            for j in range(LAG, SPP):
                step(PAIRS - 1, j)
            end = STEPS - 1
            copy_x1(end, SPP - 1)
            copy_prod(end - 1, SPP - 2)
            copy_x1t(end, SPP - 1)
            copy_prod(end, SPP - 1)

        @block.vector
        def _(dve):
            def split(t, parity, part, k):
                src = emb[:, parity, :, :].rearrange("p m d -> p d m")
                left = rest[:, :, :].rearrange("p m d -> p d m")
                if part == 0:
                    dve.wait_ge(gathered[parity], 16 * NF * (k + 1))
                    if has(t, 1):
                        dve.wait_ge(parts_turned, 2 * t)
                    nc.vector.tensor_copy(parts[:, :, 0, :], src).then_inc(hi_ready, 1)
                elif part == 1:
                    dve.wait_ge(hi_ready, t + 1)
                    nc.vector.tensor_tensor(left, src, parts[:, :, 0, :], ALU.subtract).then_inc(rest_ready, 1)
                elif part == 2:
                    dve.wait_ge(rest_ready, t + 1)
                    nc.vector.tensor_copy(parts[:, :, 1, :], left).then_inc(mid_ready, 1)
                else:
                    dve.wait_ge(mid_ready, t + 1)
                    nc.vector.tensor_tensor(parts[:, :, 2, :], left, parts[:, :, 1, :],
                                            ALU.subtract).then_inc(parts_ready, 1)

            def multiply_fields(s, j, c):
                n = CHUNKS * s + c
                dve.wait_ge(second_picked, n + 1)
                if c == 0:
                    dve.wait_ge(first_ready, s + 1)
                if not isinstance(n, int) or n >= ZBUFS:
                    dve.wait_ge(z_used, n - ZBUFS + 1)
                nc.vector.tensor_tensor(z[0:KROWS[c], n_static(j, c) % ZBUFS, :],
                                        second_ps[n_static(j, c) % 2][0:KROWS[c], :],
                                        first[0:KROWS[c], j % 2, :], ALU.mult).then_inc(z_ready, 1)

            def n_static(j, c):
                return CHUNKS * j + c

            def spread_x(s, j):
                dve.wait_ge(x_turned, s + 1)
                for b in range(OWNERS):
                    last = nc.vector.tensor_scalar(xb[:, j % 4, :, b, 0:NF],
                                                   work_ps[:, 0:GROUPS * NF].rearrange("p (g m) -> p g m", g=GROUPS),
                                                   own[:, b:b + 1], None, ALU.mult)
                last.then_inc(xb_ready, 1)

            def step(k, j):
                s = SPP * k + j
                tile = 2 * k + j // SPT
                for c in range(CHUNKS):
                    multiply_fields(s, j, c)
                    if c < 4 and opens_tile(s, j):
                        later = j // SPT + 1
                        split(tile + 1, later % 2, c, k + later // 2)
                    if c == 2:
                        spread_x(s, j)

            def mlp(k):
                dve.wait_ge(out2_done, k + 1)
                nc.vector.tensor_copy(out2[:, :], prod_ps[:, 0, 0:PAIR]).then_inc(out2_ready, 1)
                dve.wait_ge(h1_done, k + 1)
                for i in range(H1 // P):
                    last = nc.vector.tensor_scalar(h1[:, i, :], prod_ps[:, 1 + i // 2, (i % 2) * PAIR:(i % 2 + 1) * PAIR],
                                                   b1_sb[:, i:i + 1], 0.0, ALU.add, ALU.max)
                last.then_inc(h1_ready, 1)
                dve.wait_ge(h2_done, k + 1)
                for i in range(H2 // P):
                    last = nc.vector.tensor_scalar(h2[:, i, :], prod_ps[:, 3, i * PAIR:(i + 1) * PAIR],
                                                   b2_sb[:, i:i + 1], 0.0, ALU.add, ALU.max)
                last.then_inc(h2_ready, 1)
                dve.wait_ge(y_done, k + 1)
                nc.vector.tensor_copy(y[0:1, :], prod_ps[0:1, 0, 0:PAIR]).then_inc(y_ready, 1)

            nc.vector.memset(y[0:1, :], 0.0).then_inc(y_ready, 1)
            dve.wait_ge(consts_loaded, 16 * CONSTS)
            nc.vector.tensor_copy(eye_bf[:, :], eye[:, :])
            nc.vector.tensor_copy(stack[0:ROWS, :], stack_f[0:ROWS, :])
            nc.vector.tensor_copy(select[0:ROWS, :, :], select_f[0:ROWS, :, :])
            for i in range(4):
                for g in range(GROUPS):
                    last = nc.vector.tensor_copy(xb[:, i, g, :, NF], own[:, :])
            last.then_inc(consts_ready, 1)
            dve.wait_ge(ws_loaded, 32)
            nc.vector.tensor_tensor(ws[0:ROWS, :, :], ws_a[0:ROWS, :, :], ws_b[0:ROWS, :, :],
                                    ALU.add).then_inc(ws_ready, 1)
            for part in range(4):
                split(0, 0, part, 0)
            for j in range(LAG):
                step(0, j)
            dve.wait_ge(late_loaded, 16 * LATE)
            with dve.Fori(0, PAIRS - 1) as k:
                for j in range(LAG, LAG + SPP):
                    step(k, j)
                mlp(k)
            for j in range(LAG, SPP):
                step(PAIRS - 1, j)
            mlp(PAIRS - 1)


def kernel(**inputs):
    import concourse.bacc as bacc
    from concourse.bass_utils import run_bass_kernel_spmd

    nc = bacc.Bacc("TRN2", target_bir_lowering=False, num_devices=1)
    arrays = {}

    def given(name, a):
        name = "in_" + name
        arrays[name] = np.ascontiguousarray(a)
        return nc.dram_tensor(name, arrays[name].shape, mybir.dt.from_np(arrays[name].dtype),
                              kind="ExternalInput").ap()

    ids = np.asarray(inputs["ids"]).reshape(TILES, SPT, STRIPS, GROUPS, OWNERS, NF)
    ids = ids.transpose(1, 3, 2, 4, 0, 5).reshape(P, TILES * NF)

    w0 = np.asarray(inputs["L0_rec_W0"]).reshape(NF, NF, NO)
    w0a = np.zeros((ROWS, CHUNKS, NO), np.float32)
    w0b = np.zeros((ROWS, CHUNKS, NO), np.float32)
    fields = np.arange(NF)
    for shift in range(SHIFTS):
        rows = slice((shift % 3) * NF, (shift % 3 + 1) * NF)
        w0a[rows, shift // 3] = w0[fields, (fields + shift) % NF]
        if shift:
            w0b[rows, shift // 3] = w0[(fields + shift) % NF, fields]

    wt1 = np.asarray(inputs["W_top1"])
    select, stack, own, eye = constants()
    args = [given("ids", ids), [given(f"tbl_{f}", inputs[f"tbl_{f}"]) for f in range(NF)],
            given("dense", np.asarray(inputs["dense_ctx"]).T),
            given("w0a", w0a), given("w0b", w0b), given("w1", inputs["L0_rec_W1"]),
            given("wt1", wt1[:2 * NO]), given("wt1d", wt1[2 * NO:]), given("wt2", inputs["W_top2"]),
            given("wt3", np.asarray(inputs["W_top3"]).reshape(H2 // P, P).T),
            given("b1", np.asarray(inputs["b_top1"]).reshape(H1 // P, P).T),
            given("b2", np.asarray(inputs["b_top2"]).reshape(H2 // P, P).T),
            given("select", select), given("stack", stack), given("own", own), given("eye", eye)]
    out = nc.dram_tensor("out_y", (BATCH, 1), F32, kind="ExternalOutput").ap()
    build(nc, *args, out)
    r = run_bass_kernel_spmd(nc, [arrays], core_ids=[0])
    return r.results[0]["out_y"]
```

```python
from contextlib import ExitStack

import numpy as np

import concourse.bass as bass
from concourse import mybir

F32 = mybir.dt.float32
F32R = mybir.dt.float32r
BF16 = mybir.dt.bfloat16
I32 = mybir.dt.int32
U32 = mybir.dt.uint32
ALU = mybir.AluOpType
ACT = mybir.ActivationFunctionType

P = 128
BATCH = 1024
NF = 39
D = 16
NO = 128
ND = 16
H1, H2 = 512, 256

TILE = P
TILES = BATCH // TILE
STEP = 32
COLS = STEP * D
SPT = TILE // STEP
STEPS = BATCH // STEP
PAIR = 2 * TILE
PAIRS = BATCH // PAIR
SPP = PAIR // STEP
GROUPS = COLS // P
STRIPS = 2
OWNERS = 4

SHIFTS = NF // 2 + 1
ROWS = 3 * NF
CHUNKS = -(-SHIFTS // 3)
KROWS = [min(SHIFTS - 3 * c, 3) * NF for c in range(CHUNKS)]
NM = NF + 1
RING = 4
AHEAD = 3
LAG = 2
TURN = SPT - 2
SLICES = -(-NF // 2)
ENTRIES = SPP * CHUNKS + SLICES
L2_STEP = SPP + 1
TAIL_CHUNK = 4
HEAD = L2_STEP + 4 - SPP + 1
assert ENTRIES % RING == 0 and SPP * CHUNKS % RING == 0 and LAG <= HEAD <= SPP


def constants():
    select = np.zeros((3, NF, 1 + CHUNKS, ROWS), np.float32)
    for row in range(ROWS):
        m, j = row % NF, row // NF
        select[:, m, 0, row] = 1
        for c in range(CHUNKS):
            if row < KROWS[c]:
                select[:, (m + 3 * c + j) % NF, 1 + c, row] = 1
    stack = np.zeros((3, NF, NF), np.float32)
    stack[:, range(NF), range(NF)] = 1
    own = np.zeros((STRIPS, OWNERS, D, OWNERS), np.float32)
    own[:, range(OWNERS), :, range(OWNERS)] = 1
    return (select.reshape(ROWS, 1 + CHUNKS, ROWS), stack.reshape(ROWS, NF),
            own.reshape(P, OWNERS), np.eye(P, dtype=np.float32))


def build(nc, ids, tables, dense, w0a, w0b, w1, wt1, wt1d, wt2, wt3, b1, b2,
          select_d, stack_d, own_d, eye_d, out):
    with ExitStack() as ctx:
        def sb(name, shape, dt=F32):
            return ctx.enter_context(nc.sbuf_tensor(name, shape, dt))

        def bank(name, *shape):
            return ctx.enter_context(nc.psum_tensor(name, [P, *shape], F32))

        def sem(name):
            return ctx.enter_context(nc.semaphore(name))

        idx = sb("idx", [P, 2, NF], I32)
        select = sb("select", [P, 1 + CHUNKS, ROWS], BF16)
        stack = sb("stack", [P, NF], BF16)
        own = sb("own", [P, OWNERS])
        eye = sb("eye", [P, P])
        eye_bf = sb("eye_bf", [P, P], BF16)
        select_f = sb("select_f", [P, 1 + CHUNKS, ROWS])
        stack_f = sb("stack_f", [P, NF])
        ws_a = sb("ws_a", [P, CHUNKS, NO])
        ws_b = sb("ws_b", [P, CHUNKS, NO])
        ws_h = sb("ws_h", [P, CHUNKS, NO], F32R)
        ws_l = sb("ws_l", [P, CHUNKS, NO], F32R)
        w1_h = sb("w1_h", [P, NF, NO], F32R)
        w1_l = sb("w1_l", [P, NF, NO], F32R)
        wt1_sb = sb("wt1_sb", [P, 2, H1])
        wt1d_sb = sb("wt1d_sb", [P, H1])
        wt2_sb = sb("wt2_sb", [P, H1 // P, H2])
        wt3_sb = sb("wt3_sb", [P, H2 // P])
        b1_sb = sb("b1_sb", [P, H1 // P])
        b2_sb = sb("b2_sb", [P, H2 // P])
        dense_sb = sb("dense_sb", [P, PAIR])

        emb = sb("emb", [P, 2, NF, D])
        rest = sb("rest", [P, NF, D])
        parts = sb("parts", [P, D, 3, NF], BF16)
        x3 = sb("x3", [P, 2, TILE, D], BF16)
        first = sb("first", [P, 2, COLS])
        ring_h = sb("ring_h", [P, RING, COLS], F32R)
        ring_l = sb("ring_l", [P, RING, COLS], F32R)
        xb = sb("xb", [P, 4, GROUPS, OWNERS, NM])
        x1 = sb("x1", [P, 2, COLS])
        x1t = sb("x1t", [P, 2, GROUPS, NO])
        prod = sb("prod", [P, NM, PAIR])
        out1 = sb("out1", [P, PAIR])
        out2 = sb("out2", [P, PAIR])
        h1 = sb("h1", [P, H1 // P, PAIR])
        h2 = sb("h2", [P, H2 // P, PAIR])
        y = sb("y", [1, PAIR])
        w1_stage = prod[:, :, :].rearrange("p m b -> p (m b)")[:, 0:NF * NO]

        z_ps = [bank(f"z_ps{i}", COLS) for i in range(RING)]
        work_ps = bank("work_ps", COLS)
        x1_ps = bank("x1_ps", COLS)
        prod_ps = bank("prod_ps", STRIPS, 512)
        x_ps = prod_ps[:, 0, 2 * OWNERS * NM:2 * OWNERS * NM + GROUPS * NF]

        idx_loaded = [sem(f"idx_loaded{i}") for i in range(2)]
        consts_loaded = sem("consts_loaded")
        ws_loaded = sem("ws_loaded")
        w1_loaded = sem("w1_loaded")
        late_loaded = sem("late_loaded")
        dense_loaded = sem("dense_loaded")
        gathered = [sem(f"gathered{i}") for i in range(2)]
        consts_ready = sem("consts_ready")
        ws_summed = sem("ws_summed")
        weights_high = sem("weights_high")
        weights_ready = sem("weights_ready")
        hi_ready = sem("hi_ready")
        rest_ready = sem("rest_ready")
        mid_ready = sem("mid_ready")
        parts_ready = sem("parts_ready")
        parts_turned = sem("parts_turned")
        x3_ready = sem("x3_ready")
        first_picked = sem("first_picked")
        first_ready = sem("first_ready")
        second_picked = sem("second_picked")
        z_made = sem("z_made")
        high_ready = sem("high_ready")
        low_ready = sem("low_ready")
        entry_used = sem("entry_used")
        x_turned = sem("x_turned")
        xb_ready = sem("xb_ready")
        x1_ready = sem("x1_ready")
        x1_turned = sem("x1_turned")
        x1t_ready = sem("x1t_ready")
        prod_done = sem("prod_done")
        prod_ready = sem("prod_ready")
        out1_ready = sem("out1_ready")
        out2_ready = sem("out2_ready")
        h1_done = sem("h1_done")
        h1_ready = sem("h1_ready")
        h2_done = sem("h2_done")
        h2_ready = sem("h2_ready")
        y_done = sem("y_done")
        y_ready = sem("y_ready")
        y_free = sem("y_free")

        CONSTS = 4
        LATE = 6

        def has(s, low=0):
            return not isinstance(s, int) or low <= s < STEPS

        def turns_tile(k, j):
            return j % SPT == TURN and has(SPP * k + j + SPT)

        def ends_tile(k, j):
            return j % SPT == SPT - 1 and has(SPP * k + j + 1)

        def entry(k, j, c):
            return ENTRIES * k + CHUNKS * j + c + (SLICES if (j, c) > (L2_STEP, TAIL_CHUNK) else 0)

        def slice_entry(k, q):
            if isinstance(k, int):
                return entry(k, SPP - 1, CHUNKS - 1) + 1 + q
            return entry(k, L2_STEP, TAIL_CHUNK) + 1 + q

        def slice_slot(k, q):
            return slice_entry(k if isinstance(k, int) else 0, q) % RING if isinstance(k, int) \
                else (CHUNKS * L2_STEP + TAIL_CHUNK + 1 + q) % RING


        block = ctx.enter_context(nc.Block())

        @block.sync
        def _(sp):
            for t in range(2):
                sp.dma_start(idx[:, t, :], ids[:, t * NF:(t + 1) * NF]).then_inc(idx_loaded[t], 16)
            sp.dma_start(ws_a[0:ROWS, :, :], w0a).then_inc(ws_loaded, 16)
            sp.dma_start(ws_b[0:ROWS, :, :], w0b).then_inc(ws_loaded, 16)
            sp.dma_start(w1_stage.rearrange("p (m o) -> p m o", o=NO),
                         w1.rearrange("(m n) o -> n m o", n=NO)).then_inc(w1_loaded, 16)
            sp.dma_start(eye[:, :], eye_d).then_inc(consts_loaded, 16)
            sp.dma_start(select_f[0:ROWS, :, :], select_d).then_inc(consts_loaded, 16)
            sp.dma_start(stack_f[0:ROWS, :], stack_d).then_inc(consts_loaded, 16)
            sp.dma_start(own[:, :], own_d).then_inc(consts_loaded, 16)
            sp.dma_start(wt1_sb[:, :, :], wt1.rearrange("(c p) h -> p c h", p=P)).then_inc(late_loaded, 16)
            sp.dma_start(wt1d_sb[0:ND, :], wt1d).then_inc(late_loaded, 16)
            sp.dma_start(wt2_sb[:, :, :], wt2.rearrange("(c p) h -> p c h", p=P)).then_inc(late_loaded, 16)
            sp.dma_start(wt3_sb[:, :], wt3).then_inc(late_loaded, 16)
            sp.dma_start(b1_sb[:, :], b1).then_inc(late_loaded, 16)
            sp.dma_start(b2_sb[:, :], b2).then_inc(late_loaded, 16)

            sp.dma_start(dense_sb[0:ND, :], dense[:, 0:PAIR]).then_inc(dense_loaded, 16)
            with sp.Fori(1, PAIRS) as k:
                for parity in range(2):
                    sp.wait_ge(gathered[parity], 16 * NF * k)
                    sp.dma_start(idx[:, parity, :], ids[:, bass.ds((2 * k + parity) * NF, NF)]
                                 ).then_inc(idx_loaded[parity], 16)
            sp.wait_ge(y_free, 16 * PAIRS + 16)

        @block.gpsimd
        def _(pool):
            def gather(k, parity):
                pool.wait_ge(idx_loaded[parity], 16 * k + 16)
                pool.nop(nofuse=True)
                for f in range(NF):
                    pool.indirect_dma_start(
                        emb[:, parity, f, :], None, tables[f],
                        bass.IndirectOffsetOnAxis(ap=idx[:, parity, f:f + 1].bitcast(U32), axis=0),
                    ).then_inc(gathered[parity], 16)

            gather(0, 0)
            gather(0, 1)
            with pool.Fori(1, PAIRS) as k:
                for parity in range(2):
                    pool.wait_ge(rest_ready, 2 * k + parity - 1)
                    gather(k, parity)

        @block.tensor
        def _(pe):
            def columns(j):
                u = j % SPP
                v = x3[0:ROWS, u // SPT, (u % SPT) * STEP:(u % SPT + 1) * STEP, :]
                return v.rearrange("p b d -> p (b d)")

            def turn_parts(t, half):
                if half == 0:
                    pe.wait_ge(parts_ready, t + 1)
                dst = work_ps[:, :].bitcast(BF16)
                for i in range(8):
                    last = nc.tensor.transpose(dst[0:ROWS, i * P:(i + 1) * P],
                                               parts[:, 8 * half + i, :, :].rearrange("p a m -> p (a m)"),
                                               eye_bf[:, :])
                last.then_inc(parts_turned, 1)

            def pick_first(j):
                nc.tensor.matmul(work_ps[0:ROWS, :], select[0:ROWS, 0, :], columns(j),
                                 start=True, stop=True).then_inc(first_picked, 1)

            def pick_second(j, c):
                nc.tensor.matmul(z_ps[(CHUNKS * j + c) % RING][0:KROWS[c], :],
                                 select[0:ROWS, 1 + c, 0:KROWS[c]], columns(j),
                                 start=True, stop=True).then_inc(second_picked, 1)

            def three_passes(dst, w_high, w_low, high, low, start, stop):
                nc.tensor.matmul(dst, w_high, high, start=start, stop=False)
                nc.tensor.matmul(dst, w_high, low, start=False, stop=False)
                return nc.tensor.matmul(dst, w_low, high, start=False, stop=stop)

            def layer1(k, j, c):
                s, n, slot, rows = SPP * k + j, entry(k, j, c), (CHUNKS * j + c) % RING, slice(0, KROWS[c])
                pe.wait_ge(low_ready, n + 1)
                if c == 0 and has(s, 1):
                    pe.wait_ge(x1_ready, s)
                three_passes(x1_ps[:, :], ws_h[rows, c, :], ws_l[rows, c, :], ring_h[rows, slot, :],
                             ring_l[rows, slot, :], c == 0, c == CHUNKS - 1).then_inc(entry_used, 1)

            def turn_x1(s, j):
                pe.wait_ge(x1_ready, s + 1)
                for g in range(GROUPS):
                    last = nc.tensor.transpose(work_ps[:, g * P:(g + 1) * P],
                                               x1[:, j % 2, g * P:(g + 1) * P], eye[:, :])
                last.then_inc(x1_turned, 1)

            def turn_x(j):
                for g in range(GROUPS):
                    last = nc.tensor.matmul(x_ps[:, g * NF:(g + 1) * NF], columns(j)[:, g * P:(g + 1) * P],
                                            stack[0:ROWS, :], start=True, stop=True)
                last.then_inc(x_turned, 1)

            def multiply_layers(s, j, half):
                if half == 0:
                    pe.wait_ge(x1t_ready, s + 1)
                    if has(s, 1):
                        pe.wait_ge(prod_ready, 2 * s)
                for i in range(2):
                    g = 2 * half + i
                    for q in range(STRIPS):
                        r = slice(64 * q, 64 * q + 64)
                        last = nc.tensor.matmul(prod_ps[:, q, i * OWNERS * NM:(i + 1) * OWNERS * NM],
                                                x1t[r, j % 2, g, :],
                                                xb[r, j % 4, g, :, :].rearrange("p b m -> p (b m)"),
                                                start=True, stop=True)
                last.then_inc(prod_done, 1)

            def layer2(k):
                pe.wait_ge(prod_ready, 2 * (SPP * k + SPP))
                for q in range(SLICES):
                    pe.wait_ge(low_ready, slice_entry(k, q) + 1)
                    fields = min(2, NF - 2 * q)
                    for i in range(fields):
                        m, slot, b = 2 * q + i, slice_slot(k, q), slice(i * PAIR, (i + 1) * PAIR)
                        last = three_passes(prod_ps[:, 0, 0:PAIR], w1_h[:, m, :], w1_l[:, m, :],
                                            ring_h[:, slot, b], ring_l[:, slot, b], m == 0, m == NF - 1)
                    last.then_inc(entry_used, 1)

            def mlp1(k, half):
                if half == 0:
                    pe.wait_ge(dense_loaded, 16 * k + 16)
                    pe.wait_ge(out1_ready, k + 1)
                    pe.wait_ge(out2_ready, k + 1)
                for i in range(2):
                    o = prod_ps[:, half, i * PAIR:(i + 1) * PAIR]
                    cols = slice((2 * half + i) * P, (2 * half + i + 1) * P)
                    nc.tensor.matmul(o, wt1_sb[:, 0, cols], out1[:, :], start=True, stop=False)
                    nc.tensor.matmul(o, wt1d_sb[0:ND, cols], dense_sb[0:ND, :], start=False, stop=False)
                    last = nc.tensor.matmul(o, wt1_sb[:, 1, cols], out2[:, :], start=False, stop=True)
                last.then_inc(h1_done, 1)

            def mlp2(k):
                pe.wait_ge(h1_ready, 2 * k + 2)
                for j in range(H2 // P):
                    for i in range(H1 // P):
                        last = nc.tensor.matmul(prod_ps[:, 0, j * PAIR:(j + 1) * PAIR],
                                                wt2_sb[:, i, j * P:(j + 1) * P], h1[:, i, :],
                                                start=(i == 0), stop=(i == H1 // P - 1))
                last.then_inc(h2_done, 1)

            def mlp3(k):
                pe.wait_ge(h2_ready, k + 1)
                for j in range(H2 // P):
                    last = nc.tensor.matmul(prod_ps[0:1, 1, 0:PAIR], wt3_sb[:, j:j + 1], h2[:, j, :],
                                            start=(j == 0), stop=(j == H2 // P - 1))
                last.then_inc(y_done, 1)

            def wait_tail_copied(k, j):
                if j == L2_STEP + 1:
                    pe.wait_ge(out2_ready, k + 1)
                elif j in (L2_STEP + 2, L2_STEP + 3):
                    pe.wait_ge(h1_ready, 2 * k + j - L2_STEP - 1)
                elif j == L2_STEP + 4:
                    pe.wait_ge(h2_ready, k + 1)

            def step(k, j):
                s = SPP * k + j
                tile = 2 * k + j // SPT
                for c in range(CHUNKS):
                    if c + AHEAD < CHUNKS:
                        pick_second(j, c + AHEAD)
                    elif has(s + 1):
                        if c + AHEAD == CHUNKS and ends_tile(k, j):
                            pe.wait_ge(x3_ready, 2 * tile + 4)
                        pick_second(j + 1, c + AHEAD - CHUNKS)
                    if c == 0 and has(s, LAG):
                        pe.wait_ge(xb_ready, s)
                        wait_tail_copied(k, j)
                        multiply_layers(s - LAG, j - LAG, 0)
                    if c == 2:
                        if has(s, LAG):
                            pe.wait_ge(prod_ready, 2 * (s - LAG) + 1)
                            turn_x(j)
                            multiply_layers(s - LAG, j - LAG, 1)
                        else:
                            if has(s, 1):
                                pe.wait_ge(xb_ready, s)
                            turn_x(j)
                    layer1(k, j, c)
                    if c == 0 and has(s, 1):
                        if turns_tile(k, j - 1):
                            pe.wait_ge(x3_ready, 2 * tile + 3)
                        else:
                            pe.wait_ge(first_ready, s + 1)
                        turn_x1(s - 1, j - 1)
                    if c == 2 and turns_tile(k, j - 1):
                        pe.wait_ge(x1t_ready, s)
                        turn_parts(tile + 1, 1)
                    if c == (3 if turns_tile(k, j - 1) else 2) and has(s + 1):
                        if turns_tile(k, j - 1):
                            pe.wait_ge(x3_ready, 2 * tile + 4)
                        elif has(s, 1):
                            pe.wait_ge(x1t_ready, s)
                        else:
                            pe.wait_ge(first_ready, s + 1)
                        pick_first(j + 1)
                    if c == 5 and turns_tile(k, j):
                        pe.wait_ge(first_ready, s + 2)
                        turn_parts(tile + 1, 0)
                    if c == TAIL_CHUNK and L2_STEP <= j <= L2_STEP + 4:
                        pe.wait_ge(xb_ready, s + 1)
                        pe.wait_ge(prod_ready, 2 * (s - LAG) + 2)
                        if j == L2_STEP:
                            layer2(k)
                        elif j <= L2_STEP + 2:
                            mlp1(k, j - L2_STEP - 1)
                        elif j == L2_STEP + 3:
                            mlp2(k)
                        else:
                            mlp3(k)
                    if (j, c) == (L2_STEP + 4, CHUNKS - 1):
                        pe.wait_ge(y_ready, k + 1)

            pe.wait_ge(consts_ready, 1)
            turn_parts(0, 0)
            pe.wait_ge(x3_ready, 1)
            turn_parts(0, 1)
            pe.wait_ge(x3_ready, 2)
            pick_first(0)
            for c in range(AHEAD):
                pick_second(0, c)
            pe.wait_ge(weights_ready, 2)
            for j in range(HEAD):
                step(0, j)
            pe.wait_ge(late_loaded, 16 * LATE)
            with pe.Fori(0, PAIRS - 1) as k:
                for j in range(HEAD, HEAD + SPP):
                    step(k, j)
            for j in range(HEAD, SPP):
                step(PAIRS - 1, j)
            end = STEPS - 1
            pe.wait_ge(xb_ready, end + 1)
            multiply_layers(end - 1, SPP - 2, 0)
            turn_x1(end, SPP - 1)
            pe.wait_ge(prod_ready, 2 * end - 1)
            multiply_layers(end - 1, SPP - 2, 1)
            multiply_layers(end, SPP - 1, 0)
            pe.wait_ge(prod_ready, 2 * end + 1)
            multiply_layers(end, SPP - 1, 1)
            layer2(PAIRS - 1)
            mlp1(PAIRS - 1, 0)
            mlp1(PAIRS - 1, 1)
            mlp2(PAIRS - 1)
            mlp3(PAIRS - 1)

        @block.scalar
        def _(act):
            def copy_hi(t, parity, k):
                act.wait_ge(gathered[parity], 16 * NF * (k + 1))
                if has(t, 1):
                    act.wait_ge(parts_turned, 2 * t)
                nc.scalar.copy(parts[:, :, 0, :], emb[:, parity, :, :].rearrange("p m d -> p d m")
                               ).then_inc(hi_ready, 1)

            def copy_mid(t):
                act.wait_ge(rest_ready, t + 1)
                nc.scalar.copy(parts[:, :, 1, :], rest[:, :, :].rearrange("p m d -> p d m")
                               ).then_inc(mid_ready, 1)

            def copy_parts(t, parity, half):
                act.wait_ge(parts_turned, 2 * t + half + 1)
                nc.scalar.copy(x3[0:ROWS, parity, :, 8 * half:8 * half + 8].rearrange("p b d -> p d b"),
                               work_ps[0:ROWS, :].bitcast(BF16).rearrange("p (d b) -> p d b", d=8)
                               ).then_inc(x3_ready, 1)

            def copy_first(s, j):
                act.wait_ge(first_picked, s + 1)
                nc.scalar.copy(first[0:ROWS, j % 2, :], work_ps[0:ROWS, :]).then_inc(first_ready, 1)

            def round_high(k, j, c):
                m, n, rows = SPP * CHUNKS * k + CHUNKS * j + c, entry(k, j, c), slice(0, KROWS[c])
                act.wait_ge(z_made, m + 1)
                if not isinstance(n, int) or n >= RING:
                    act.wait_ge(entry_used, n - RING + 1)
                slot = (CHUNKS * j + c) % RING
                nc.scalar.copy(ring_h[rows, slot, :], z_ps[slot][rows, :]).then_inc(high_ready, 1)

            def round_slice(k, q):
                n, fields = slice_entry(k, q), min(2, NF - 2 * q)
                act.wait_ge(entry_used, n - RING + 1)
                nc.scalar.copy(ring_h[:, slice_slot(k, q), 0:fields * PAIR],
                               prod[:, 2 * q:2 * q + fields, :].rearrange("p m b -> p (m b)")
                               ).then_inc(high_ready, 1)

            def copy_x1(s, k, j):
                act.wait_ge(entry_used, entry(k, j, CHUNKS - 1) + 1)
                nc.scalar.copy(x1[:, j % 2, :], x1_ps[:, :]).then_inc(x1_ready, 1)

            def copy_x1t(s, j):
                act.wait_ge(x1_turned, s + 1)
                nc.scalar.copy(x1t[:, j % 2, :, :].rearrange("p g n -> p (g n)"),
                               work_ps[:, :]).then_inc(x1t_ready, 1)

            def spread_x(s, j, half):
                act.wait_ge(x_turned, s + 1)
                for b in range(OWNERS // 2 * half, OWNERS // 2 * half + OWNERS // 2):
                    last = nc.scalar.activation(xb[:, j % 4, :, b, 0:NF],
                                                x_ps.rearrange("p (g m) -> p g m", g=GROUPS),
                                                ACT.Copy, scale=own[:, b:b + 1])
                if half == 1:
                    last.then_inc(xb_ready, 1)

            def copy_prod(s, j, half):
                act.wait_ge(prod_done, 2 * s + half + 1)
                b = (j % SPP) * STEP + half * (STEP // 2)
                nc.scalar.copy(prod[:, :, b:b + STEP // 2].rearrange("p m (q b) -> p q b m", q=STRIPS),
                               prod_ps[:, :, 0:2 * OWNERS * NM].rearrange("p q (b m) -> p q b m", m=NM)
                               ).then_inc(prod_ready, 1)

            def slices(k):
                act.wait_ge(prod_ready, 2 * (SPP * k + SPP))
                nc.scalar.copy(out1[:, :], prod[:, NF, :]).then_inc(out1_ready, 1)
                for q in range(SLICES):
                    round_slice(k, q)

            def copy_out2(k):
                act.wait_ge(entry_used, slice_entry(k, SLICES - 1) + 1)
                nc.scalar.copy(out2[:, :], prod_ps[:, 0, 0:PAIR]).then_inc(out2_ready, 1)

            def relu1(k, half):
                act.wait_ge(h1_done, 2 * k + half + 1)
                for i in range(2):
                    last = nc.scalar.activation(h1[:, 2 * half + i, :], prod_ps[:, half, i * PAIR:(i + 1) * PAIR],
                                                ACT.Relu, bias=b1_sb[:, 2 * half + i:2 * half + i + 1])
                last.then_inc(h1_ready, 1)

            def relu2(k):
                act.wait_ge(h2_done, k + 1)
                for i in range(H2 // P):
                    last = nc.scalar.activation(h2[:, i, :], prod_ps[:, 0, i * PAIR:(i + 1) * PAIR],
                                                ACT.Relu, bias=b2_sb[:, i:i + 1])
                last.then_inc(h2_ready, 1)

            def copy_y(k):
                act.wait_ge(y_done, k + 1)
                act.wait_ge(y_free, 16 * k + 16)
                nc.scalar.copy(y[0:1, :], prod_ps[0:1, 1, 0:PAIR]).then_inc(y_ready, 1)
                act.wait_ge(y_ready, k + 1)
                act.dma_start(out[bass.ds(k * PAIR, PAIR), :].rearrange("b a -> a b"),
                              y[0:1, :]).then_inc(y_free, 16)

            def step(k, j):
                s = SPP * k + j
                tile = 2 * k + j // SPT
                nxt = j // SPT + 1
                for c in range(CHUNKS):
                    round_high(k, j, c)
                    if c == 0 and j in (L2_STEP + 2, L2_STEP + 3):
                        relu1(k, j - L2_STEP - 2)
                    if c == 0 and j == L2_STEP + 4:
                        relu2(k)
                    if c == 1 and turns_tile(k, j - 1):
                        copy_parts(tile + 1, nxt % 2, 0)
                    if c == 1 and has(s, 1):
                        copy_x1(s - 1, k, j - 1)
                    if c == 2 and has(s, LAG):
                        copy_prod(s - LAG, j - LAG, 0)
                    if c == 2 and turns_tile(k, j):
                        copy_hi(tile + 1, nxt % 2, k + nxt // 2)
                    if c == 3 and has(s, 1):
                        copy_x1t(s - 1, j - 1)
                    if c == 4:
                        if has(s, LAG):
                            copy_prod(s - LAG, j - LAG, 1)
                        spread_x(s, j, 0)
                    if c == (4 if j == L2_STEP else 5):
                        spread_x(s, j, 1)
                    if (j, c) == (L2_STEP, TAIL_CHUNK):
                        slices(k)
                    if c == 5 and turns_tile(k, j):
                        copy_mid(tile + 1)
                    if c == 5 and turns_tile(k, j - 1):
                        copy_parts(tile + 1, nxt % 2, 1)
                    if c == (6 if turns_tile(k, j - 1) else 5) and has(s + 1):
                        copy_first(s + 1, j + 1)
                    if (j, c) == (L2_STEP, 5):
                        copy_out2(k)
                    if (j, c) == (L2_STEP + 4, CHUNKS - 1):
                        copy_y(k)
                        act.dma_start(dense_sb[0:ND, :], dense[:, bass.ds((k + 1) * PAIR, PAIR)]
                                      ).then_inc(dense_loaded, 16)

            act.wait_ge(ws_summed, 1)
            nc.scalar.copy(ws_h[0:ROWS, :, :], ws_a[0:ROWS, :, :]).then_inc(weights_high, 1)
            act.wait_ge(w1_loaded, 16)
            nc.scalar.copy(w1_h[:, :, :].rearrange("p m o -> p (m o)"), w1_stage).then_inc(weights_high, 1)
            copy_hi(0, 0, 0)
            copy_mid(0)
            copy_parts(0, 0, 0)
            copy_parts(0, 0, 1)
            copy_first(0, 0)
            for j in range(HEAD):
                step(0, j)
            with act.Fori(0, PAIRS - 1) as k:
                for j in range(HEAD, HEAD + SPP):
                    step(k, j)
            for j in range(HEAD, SPP):
                step(PAIRS - 1, j)
            end = STEPS - 1
            copy_x1(end, PAIRS - 1, SPP - 1)
            copy_prod(end - 1, SPP - 2, 0)
            copy_x1t(end, SPP - 1)
            copy_prod(end - 1, SPP - 2, 1)
            copy_prod(end, SPP - 1, 0)
            copy_prod(end, SPP - 1, 1)
            slices(PAIRS - 1)
            copy_out2(PAIRS - 1)
            relu1(PAIRS - 1, 0)
            relu1(PAIRS - 1, 1)
            relu2(PAIRS - 1)
            copy_y(PAIRS - 1)

        @block.vector
        def _(dve):
            def split_rest(t, parity):
                dve.wait_ge(hi_ready, t + 1)
                nc.vector.tensor_tensor(rest[:, :, :].rearrange("p m d -> p d m"),
                                        emb[:, parity, :, :].rearrange("p m d -> p d m"),
                                        parts[:, :, 0, :], ALU.subtract).then_inc(rest_ready, 1)

            def split_lo(t):
                dve.wait_ge(mid_ready, t + 1)
                nc.vector.tensor_tensor(parts[:, :, 2, :], rest[:, :, :].rearrange("p m d -> p d m"),
                                        parts[:, :, 1, :], ALU.subtract).then_inc(parts_ready, 1)

            def multiply_fields(k, j, c):
                dve.wait_ge(second_picked, SPP * CHUNKS * k + CHUNKS * j + c + 1)
                if c == 0:
                    dve.wait_ge(first_ready, SPP * k + j + 1)
                bank_ps = z_ps[(CHUNKS * j + c) % RING][0:KROWS[c], :]
                nc.vector.tensor_tensor(bank_ps, bank_ps, first[0:KROWS[c], j % 2, :],
                                        ALU.mult).then_inc(z_made, 1)

            def take_low(k, j, c):
                slot, rows = (CHUNKS * j + c) % RING, slice(0, KROWS[c])
                dve.wait_ge(high_ready, entry(k, j, c) + 1)
                nc.vector.tensor_tensor(ring_l[rows, slot, :], z_ps[slot][rows, :],
                                        ring_h[rows, slot, :], ALU.subtract).then_inc(low_ready, 1)

            def slices(k):
                for q in range(SLICES):
                    n, slot, fields = slice_entry(k, q), slice_slot(k, q), min(2, NF - 2 * q)
                    dve.wait_ge(high_ready, n + 1)
                    nc.vector.tensor_tensor(ring_l[:, slot, 0:fields * PAIR],
                                            prod[:, 2 * q:2 * q + fields, :].rearrange("p m b -> p (m b)"),
                                            ring_h[:, slot, 0:fields * PAIR],
                                            ALU.subtract).then_inc(low_ready, 1)

            def step(k, j):
                s = SPP * k + j
                tile = 2 * k + j // SPT
                nxt = j // SPT + 1
                for c in range(CHUNKS):
                    multiply_fields(k, j, c)
                    late = (k, j, c - 1) if c else (k, j - 1, CHUNKS - 1)
                    if late[1:] == (L2_STEP, TAIL_CHUNK + 1):
                        slices(k)
                    if c or has(s, 1):
                        take_low(*late)
                    if c == 4 and turns_tile(k, j):
                        split_rest(tile + 1, nxt % 2)
                    if c == 6 and turns_tile(k, j):
                        split_lo(tile + 1)

            nc.vector.memset(y[0:1, :], 0.0).then_inc(y_free, 16)
            dve.wait_ge(ws_loaded, 32)
            nc.vector.tensor_tensor(ws_a[0:ROWS, :, :], ws_a[0:ROWS, :, :], ws_b[0:ROWS, :, :],
                                    ALU.add).then_inc(ws_summed, 1)
            dve.wait_ge(weights_high, 1)
            nc.vector.tensor_tensor(ws_l[0:ROWS, :, :], ws_a[0:ROWS, :, :], ws_h[0:ROWS, :, :],
                                    ALU.subtract).then_inc(weights_ready, 1)
            dve.wait_ge(consts_loaded, 16 * CONSTS)
            nc.vector.tensor_copy(eye_bf[:, :], eye[:, :])
            nc.vector.tensor_copy(stack[0:ROWS, :], stack_f[0:ROWS, :])
            nc.vector.tensor_copy(select[0:ROWS, :, :], select_f[0:ROWS, :, :])
            for i in range(4):
                for g in range(GROUPS):
                    last = nc.vector.tensor_copy(xb[:, i, g, :, NF], own[:, :])
            last.then_inc(consts_ready, 1)
            dve.wait_ge(weights_high, 2)
            nc.vector.tensor_tensor(w1_l[:, :, :].rearrange("p m o -> p (m o)"), w1_stage,
                                    w1_h[:, :, :].rearrange("p m o -> p (m o)"),
                                    ALU.subtract).then_inc(weights_ready, 1)
            split_rest(0, 0)
            split_lo(0)
            for j in range(HEAD):
                step(0, j)
            with dve.Fori(0, PAIRS - 1) as k:
                for j in range(HEAD, HEAD + SPP):
                    step(k, j)
            for j in range(HEAD, SPP):
                step(PAIRS - 1, j)
            take_low(PAIRS - 1, SPP - 1, CHUNKS - 1)
            slices(PAIRS - 1)


def kernel(**inputs):
    import concourse.bacc as bacc
    from concourse.bass_utils import run_bass_kernel_spmd

    nc = bacc.Bacc("TRN2", target_bir_lowering=False, num_devices=1)
    arrays = {}

    def given(name, a):
        name = "in_" + name
        arrays[name] = np.ascontiguousarray(a)
        return nc.dram_tensor(name, arrays[name].shape, mybir.dt.from_np(arrays[name].dtype),
                              kind="ExternalInput").ap()

    ids = np.asarray(inputs["ids"]).reshape(TILES, P // 16, STRIPS, 2, OWNERS, NF)
    ids = ids.transpose(1, 3, 2, 4, 0, 5).reshape(P, TILES * NF)

    w0 = np.asarray(inputs["L0_rec_W0"]).reshape(NF, NF, NO)
    w0a = np.zeros((ROWS, CHUNKS, NO), np.float32)
    w0b = np.zeros((ROWS, CHUNKS, NO), np.float32)
    fields = np.arange(NF)
    for shift in range(SHIFTS):
        rows = slice((shift % 3) * NF, (shift % 3 + 1) * NF)
        w0a[rows, shift // 3] = w0[fields, (fields + shift) % NF]
        if shift:
            w0b[rows, shift // 3] = w0[(fields + shift) % NF, fields]

    wt1 = np.asarray(inputs["W_top1"])
    select, stack, own, eye = constants()
    args = [given("ids", ids), [given(f"tbl_{f}", inputs[f"tbl_{f}"]) for f in range(NF)],
            given("dense", np.asarray(inputs["dense_ctx"]).T),
            given("w0a", w0a), given("w0b", w0b), given("w1", inputs["L0_rec_W1"]),
            given("wt1", wt1[:2 * NO]), given("wt1d", wt1[2 * NO:]), given("wt2", inputs["W_top2"]),
            given("wt3", np.asarray(inputs["W_top3"]).reshape(H2 // P, P).T),
            given("b1", np.asarray(inputs["b_top1"]).reshape(H1 // P, P).T),
            given("b2", np.asarray(inputs["b_top2"]).reshape(H2 // P, P).T),
            given("select", select), given("stack", stack), given("own", own), given("eye", eye)]
    out = nc.dram_tensor("out_y", (BATCH, 1), F32, kind="ExternalOutput").ap()
    build(nc, *args, out)
    r = run_bass_kernel_spmd(nc, [arrays], core_ids=[0])
    return r.results[0]["out_y"]
```

```python
from contextlib import ExitStack

import numpy as np

import concourse.bass as bass
from concourse import mybir

F32 = mybir.dt.float32
F32R = mybir.dt.float32r
BF16 = mybir.dt.bfloat16
I32 = mybir.dt.int32
U32 = mybir.dt.uint32
ALU = mybir.AluOpType
ACT = mybir.ActivationFunctionType

P = 128
BATCH = 1024
NF = 39
D = 16
NO = 128
ND = 16
H1, H2 = 512, 256

TILE = P
TILES = BATCH // TILE
STEP = 32
COLS = STEP * D
SPT = TILE // STEP
STEPS = BATCH // STEP
PAIR = 2 * TILE
PAIRS = BATCH // PAIR
SPP = PAIR // STEP
GROUPS = COLS // P
STRIPS = 2
OWNERS = 4

PARTS = 3 * NF
PRODUCTS = NF * (NF + 1) // 2
CHUNKS = -(-PRODUCTS // P)
FULL = CHUNKS - 1
SMALL = PRODUCTS - FULL * P
KROWS = [P] * FULL + [96]
NM = NF + 1
RING = 4
AHEAD = RING
SLICES = -(-NF // 2)
ENTRIES = SPP * CHUNKS + SLICES
L2_STEP = SPP + 1
SLOTS = (1, 5)
HEAD = L2_STEP + 2 - SPP + 1
assert ENTRIES % RING == 0 and SPP * CHUNKS % RING == 0 and 2 <= HEAD <= SPP
STACKED = 96
W1_AT, WT1_AT = 0, NF * NO
WT2_AT = WT1_AT + 2 * H1
WTD_AT = WT2_AT + H1 // P * H2
WEIGHTS = WTD_AT + H1
assert WEIGHTS <= NM * PAIR


def pair_rows():
    fields = np.full(P, -1)
    for at in (0, 32, 64):
        fields[at:at + SMALL] = np.arange(SMALL)
    free = np.flatnonzero(fields < 0)
    fields[free] = SMALL + np.arange(len(free)) % (NF - SMALL)
    room = np.bincount(fields, minlength=NF) * FULL
    room[:SMALL] += 1
    owns = np.array([[(p - m) % NF <= NF // 2 for p in range(NF)] for m in range(NF)])
    while (owns.sum(1) > room).any():
        path = {int(np.argmax(owns.sum(1) - room)): None}
        for m in (queue := list(path)):
            if owns[m].sum() < room[m]:
                break
            for p in np.flatnonzero(owns[m]):
                if int(p) not in path:
                    path[int(p)] = m
                    queue.append(int(p))
        while path[m] is not None:
            owns[path[m], m], owns[m, path[m]] = False, True
            m = path[m]
    products = []
    for m in range(NF):
        rows, partners = np.flatnonzero(fields == m), np.flatnonzero(owns[m])
        for i, p in enumerate(partners):
            if i < len(rows) * FULL:
                products.append((rows[i // FULL], i % FULL, m, p))
            else:
                products += [(at + m, FULL, m, p) for at in (0, 32, 64)]
    return fields, products


def constants():
    fields, products = pair_rows()
    select = np.zeros((3, NF, 1 + CHUNKS, P), np.float32)
    select[:, fields, 0, range(P)] = 1
    for row, c, m, p in products:
        select[:, p, 1 + c, row] = 1
    stack = np.zeros((3, NF, NF), np.float32)
    stack[:, range(NF), range(NF)] = 1
    own = np.zeros((STRIPS, OWNERS, D, OWNERS), np.float32)
    own[:, range(OWNERS), :, range(OWNERS)] = 1
    return (select.reshape(PARTS, 1 + CHUNKS, P), stack.reshape(PARTS, NF),
            own.reshape(P, OWNERS), np.eye(P, dtype=np.float32))


def build(nc, ids, tables, dense, w0a, w0b, w1, wt1, wt1d, wt2, wt3, b1, b2,
          select_d, stack_d, own_d, eye_d, out):
    with ExitStack() as ctx:
        def sb(name, shape, dt=F32):
            return ctx.enter_context(nc.sbuf_tensor(name, shape, dt))

        def bank(name, *shape):
            return ctx.enter_context(nc.psum_tensor(name, [P, *shape], F32))

        def sem(name):
            return ctx.enter_context(nc.semaphore(name))

        idx = sb("idx", [P, 2, NF], I32)
        select = sb("select", [P, 1 + CHUNKS, P], BF16)
        stack = sb("stack", [P, NF], BF16)
        own = sb("own", [P, OWNERS])
        eye = sb("eye", [P, P])
        eye_bf = sb("eye_bf", [P, P], BF16)
        select_f = sb("select_f", [P, 1 + CHUNKS, P])
        stack_f = sb("stack_f", [P, NF])
        ws_a = sb("ws_a", [P, CHUNKS, NO])
        ws_b = sb("ws_b", [P, CHUNKS, NO])
        ws_h = sb("ws_h", [P, CHUNKS, NO], F32R)
        ws_l = sb("ws_l", [P, CHUNKS, NO], F32R)
        weights_h = sb("weights_h", [P, WEIGHTS], F32R)
        weights_l = sb("weights_l", [P, WEIGHTS], F32R)
        wt3_sb = sb("wt3_sb", [P, H2 // P])
        b1_sb = sb("b1_sb", [P, H1 // P])
        b2_sb = sb("b2_sb", [P, H2 // P])
        dense_sb = sb("dense_sb", [P, PAIR])
        dense_s = sb("dense_s", [P, PAIR], F32R)

        emb = sb("emb", [P, 2, NF, D])
        rest = sb("rest", [P, NF, D])
        parts = sb("parts", [P, D, 3, NF], BF16)
        x3 = sb("x3", [P, 2, TILE, D], BF16)
        first = sb("first", [P, 2, COLS])
        ring_h = sb("ring_h", [P, RING, COLS], F32R)
        ring_l = sb("ring_l", [P, RING, COLS], F32R)
        xb = sb("xb", [P, 2, GROUPS, OWNERS, NM])
        x1 = sb("x1", [P, 2, COLS])
        x1t = sb("x1t", [P, 2, GROUPS, NO])
        prod = sb("prod", [P, NM, PAIR])
        outs_h = sb("outs_h", [P, 2, PAIR], F32R)
        outs_l = sb("outs_l", [P, 2, PAIR], F32R)
        h1 = sb("h1", [P, H1 // P, PAIR])
        h1_h = sb("h1_h", [P, H1 // P, PAIR], F32R)
        h1_l = sb("h1_l", [P, H1 // P, PAIR], F32R)
        h2 = sb("h2", [P, H2 // P, PAIR])
        y = sb("y", [1, PAIR])
        stage = prod[:, :, :].rearrange("p m b -> p (m b)")[:, 0:WEIGHTS]

        z_ps = [bank(f"z_ps{i}", COLS) for i in range(RING)]
        work_ps = bank("work_ps", COLS)
        x1_ps = bank("x1_ps", COLS)
        prod_ps = bank("prod_ps", STRIPS, 512)
        x_ps = prod_ps[:, 0, 2 * OWNERS * NM:2 * OWNERS * NM + GROUPS * NF]

        idx_loaded = [sem(f"idx_loaded{i}") for i in range(2)]
        consts_loaded = sem("consts_loaded")
        ws_loaded = sem("ws_loaded")
        weights_loaded = sem("weights_loaded")
        late_loaded = sem("late_loaded")
        dense_loaded = sem("dense_loaded")
        gathered = [sem(f"gathered{i}") for i in range(2)]
        consts_ready = sem("consts_ready")
        ws_summed = sem("ws_summed")
        weights_high = sem("weights_high")
        weights_ready = sem("weights_ready")
        hi_ready = sem("hi_ready")
        rest_ready = sem("rest_ready")
        mid_ready = sem("mid_ready")
        parts_ready = sem("parts_ready")
        parts_turned = sem("parts_turned")
        x3_ready = sem("x3_ready")
        first_picked = sem("first_picked")
        first_ready = sem("first_ready")
        second_picked = sem("second_picked")
        z_made = sem("z_made")
        high_ready = sem("high_ready")
        low_ready = sem("low_ready")
        entry_used = sem("entry_used")
        x_turned = sem("x_turned")
        xb_ready = sem("xb_ready")
        x1_ready = sem("x1_ready")
        x1_turned = sem("x1_turned")
        x1t_ready = sem("x1t_ready")
        prod_done = sem("prod_done")
        prod_ready = sem("prod_ready")
        out1_high = sem("out1_high")
        out1_ready = sem("out1_ready")
        out2_high = sem("out2_high")
        out2_ready = sem("out2_ready")
        dense_high = sem("dense_high")
        dense_ready = sem("dense_ready")
        h1_done = sem("h1_done")
        h1_copied = sem("h1_copied")
        h1_high = sem("h1_high")
        h1_ready = sem("h1_ready")
        h2_done = sem("h2_done")
        h2_ready = sem("h2_ready")
        y_done = sem("y_done")
        y_ready = sem("y_ready")
        y_free = sem("y_free")

        CONSTS = 4
        WEIGHT_LOADS = 4
        LATE = 3

        def has(s, low=0):
            return not isinstance(s, int) or low <= s < STEPS

        def ends_tile(k, j):
            return j % SPT == SPT - 1 and has(SPP * k + j + 1)

        def begin_tile(j):
            return 0 if j > SPP else 1

        def entry(k, j, c):
            return ENTRIES * k + CHUNKS * j + c + (SLICES if (j, c) > (L2_STEP, SLOTS[0]) else 0)

        def slice_entry(k, q):
            if isinstance(k, int):
                return entry(k, SPP - 1, CHUNKS - 1) + 1 + q
            return entry(k, L2_STEP, SLOTS[0]) + 1 + q

        def slice_slot(k, q):
            if isinstance(k, int):
                return slice_entry(k, q) % RING
            return (CHUNKS * L2_STEP + SLOTS[0] + 1 + q) % RING

        block = ctx.enter_context(nc.Block())

        @block.sync
        def _(sp):
            for t in range(2):
                sp.dma_start(idx[:, t, :], ids[:, t * NF:(t + 1) * NF]).then_inc(idx_loaded[t], 16)
            sp.dma_start(ws_a[:, :, :], w0a).then_inc(ws_loaded, 16)
            sp.dma_start(ws_b[:, :, :], w0b).then_inc(ws_loaded, 16)
            sp.dma_start(eye[:, :], eye_d).then_inc(consts_loaded, 16)
            sp.dma_start(select_f[0:PARTS, :, :], select_d).then_inc(consts_loaded, 16)
            sp.dma_start(stack_f[0:PARTS, :], stack_d).then_inc(consts_loaded, 16)
            sp.dma_start(own[:, :], own_d).then_inc(consts_loaded, 16)
            sp.dma_start(stage[:, W1_AT:WT1_AT].rearrange("p (m o) -> p m o", o=NO),
                         w1.rearrange("(m n) o -> n m o", n=NO)).then_inc(weights_loaded, 16)
            sp.dma_start(stage[:, WT1_AT:WT2_AT].rearrange("p (c h) -> p c h", h=H1),
                         wt1.rearrange("(c p) h -> p c h", p=P)).then_inc(weights_loaded, 16)
            sp.dma_start(stage[:, WT2_AT:WTD_AT].rearrange("p (c h) -> p c h", h=H2),
                         wt2.rearrange("(c p) h -> p c h", p=P)).then_inc(weights_loaded, 16)
            sp.dma_start(stage[:, WTD_AT:WEIGHTS], wt1d).then_inc(weights_loaded, 16)
            sp.dma_start(wt3_sb[:, :], wt3).then_inc(late_loaded, 16)
            sp.dma_start(b1_sb[:, :], b1).then_inc(late_loaded, 16)
            sp.dma_start(b2_sb[:, :], b2).then_inc(late_loaded, 16)

            sp.dma_start(dense_sb[0:STACKED, :], dense[:, 0:PAIR]).then_inc(dense_loaded, 16)

            def load_idx(k):
                for parity in range(2):
                    sp.wait_ge(gathered[parity], 16 * NF * k)
                    sp.dma_start(idx[:, parity, :], ids[:, bass.ds((2 * k + parity) * NF, NF)]
                                 ).then_inc(idx_loaded[parity], 16)

            def store(k):
                sp.wait_ge(y_ready, k + 1)
                sp.dma_start(out[bass.ds(k * PAIR, PAIR), :].rearrange("b a -> a b"),
                             y[0:1, :]).then_inc(y_free, 16)

            def load_dense(k):
                sp.dma_start(dense_sb[0:STACKED, :], dense[:, bass.ds(k * PAIR, PAIR)]).then_inc(dense_loaded, 16)

            load_idx(1)
            with sp.Fori(2, PAIRS) as k:
                load_idx(k)
                store(k - 2)
                load_dense(k - 1)
            store(PAIRS - 2)
            load_dense(PAIRS - 1)
            store(PAIRS - 1)
            sp.wait_ge(y_free, 16 * PAIRS + 16)

        @block.gpsimd
        def _(pool):
            def gather(k, parity):
                pool.wait_ge(idx_loaded[parity], 16 * k + 16)
                pool.nop(nofuse=True)
                for f in range(NF):
                    pool.indirect_dma_start(
                        emb[:, parity, f, :], None, tables[f],
                        bass.IndirectOffsetOnAxis(ap=idx[:, parity, f:f + 1].bitcast(U32), axis=0),
                    ).then_inc(gathered[parity], 16)

            gather(0, 0)
            gather(0, 1)
            with pool.Fori(1, PAIRS) as k:
                for parity in range(2):
                    pool.wait_ge(rest_ready, 2 * k + parity - 1)
                    gather(k, parity)

        @block.tensor
        def _(pe):
            def columns(j):
                u = j % SPP
                v = x3[0:PARTS, u // SPT, (u % SPT) * STEP:(u % SPT + 1) * STEP, :]
                return v.rearrange("p b d -> p (b d)")

            def turn_parts(t, half):
                if half == 0:
                    pe.wait_ge(parts_ready, t + 1)
                dst = work_ps[:, :].bitcast(BF16)
                for i in range(8):
                    last = nc.tensor.transpose(dst[0:PARTS, i * P:(i + 1) * P],
                                               parts[:, 8 * half + i, :, :].rearrange("p a m -> p (a m)"),
                                               eye_bf[:, :])
                last.then_inc(parts_turned, 1)

            def pick_first(j):
                nc.tensor.matmul(work_ps[:, :], select[0:PARTS, 0, :], columns(j),
                                 start=True, stop=True).then_inc(first_picked, 1)

            def pick_second(j, c):
                nc.tensor.matmul(z_ps[(CHUNKS * j + c) % RING][0:KROWS[c], :],
                                 select[0:PARTS, 1 + c, 0:KROWS[c]], columns(j),
                                 start=True, stop=True).then_inc(second_picked, 1)

            def three_passes(dst, w_high, w_low, high, low, start, stop):
                nc.tensor.matmul(dst, w_high, high, start=start, stop=False)
                nc.tensor.matmul(dst, w_high, low, start=False, stop=False)
                return nc.tensor.matmul(dst, w_low, high, start=False, stop=stop)

            def layer1(k, j, c):
                s, slot, rows = SPP * k + j, (CHUNKS * j + c) % RING, slice(0, KROWS[c])
                if c == 0 and has(s, 1):
                    pe.wait_ge(x1_ready, s)
                if c < FULL:
                    last = three_passes(x1_ps[:, :], ws_h[:, c, :], ws_l[:, c, :], ring_h[:, slot, :],
                                        ring_l[:, slot, :], c == 0, False)
                else:
                    last = nc.tensor.matmul(x1_ps[:, :], ws_h[rows, c, :], ring_h[rows, slot, :],
                                            start=False, stop=True)
                last.then_inc(entry_used, 1)

            def turn_x1(s, j):
                pe.wait_ge(x1_ready, s + 1)
                for g in range(GROUPS):
                    last = nc.tensor.transpose(work_ps[:, g * P:(g + 1) * P],
                                               x1[:, j % 2, g * P:(g + 1) * P], eye[:, :])
                last.then_inc(x1_turned, 1)

            def turn_x(j):
                for g in range(GROUPS):
                    last = nc.tensor.matmul(x_ps[:, g * NF:(g + 1) * NF], columns(j)[:, g * P:(g + 1) * P],
                                            stack[0:PARTS, :], start=True, stop=True)
                last.then_inc(x_turned, 1)

            def multiply_layers(s, j, g, banks=None):
                if g == 0:
                    pe.wait_ge(x1t_ready, s + 1)
                    if has(s, 1):
                        pe.wait_ge(prod_ready, 2 * s)
                if g == 2 and banks is None:
                    pe.wait_ge(prod_ready, 2 * s + 1)
                for q in range(STRIPS):
                    r = slice(64 * q, 64 * q + 64)
                    at = slice((g % 2) * OWNERS * NM, (g % 2 + 1) * OWNERS * NM)
                    last = nc.tensor.matmul(banks[q][:, at] if banks else prod_ps[:, q, at],
                                            x1t[r, j % 2, g, :],
                                            xb[r, j % 2, g, :, :].rearrange("p b m -> p (b m)"),
                                            start=True, stop=True)
                if g % 2:
                    last.then_inc(prod_done, 1)

            def layer2(k):
                pe.wait_ge(prod_ready, 2 * (SPP * k + SPP))
                for q in range(SLICES):
                    pe.wait_ge(low_ready, slice_entry(k, q) + 1)
                    fields = min(2, NF - 2 * q)
                    for i in range(fields):
                        m, slot, b = 2 * q + i, slice_slot(k, q), slice(i * PAIR, (i + 1) * PAIR)
                        last = three_passes(prod_ps[:, 0, 0:PAIR], weights_h[:, m * NO:(m + 1) * NO],
                                            weights_l[:, m * NO:(m + 1) * NO],
                                            ring_h[:, slot, b], ring_l[:, slot, b], m == 0, m == NF - 1)
                    last.then_inc(entry_used, 1)

            def mlp1(k, half):
                if half == 0:
                    pe.wait_ge(out1_ready, k + 1)
                    pe.wait_ge(dense_ready, k + 1)
                for i in range(2):
                    o, at = prod_ps[:, 1 - half, i * PAIR:(i + 1) * PAIR], (2 * half + i) * P
                    nc.tensor.matmul(o, weights_h[0:STACKED, WTD_AT + at:WTD_AT + at + P],
                                     dense_s[0:STACKED, :], start=True, stop=False)
                    for layer in range(2):
                        if (half, i, layer) == (0, 0, 1):
                            pe.wait_ge(out2_ready, k + 1)
                        cols = slice(WT1_AT + layer * H1 + at, WT1_AT + layer * H1 + at + P)
                        last = three_passes(o, weights_h[:, cols], weights_l[:, cols],
                                            outs_h[:, layer, :], outs_l[:, layer, :], False, layer == 1)
                last.then_inc(h1_done, 1)

            def mlp2(k):
                for j in range(H2 // P):
                    for i in range(H1 // P):
                        if j == 0 and i % 2 == 0:
                            pe.wait_ge(h1_ready, 2 * k + i // 2 + 1)
                        cols = slice(WT2_AT + i * H2 + j * P, WT2_AT + i * H2 + (j + 1) * P)
                        last = three_passes(prod_ps[:, 1 - j, 0:PAIR], weights_h[:, cols], weights_l[:, cols],
                                            h1_h[:, i, :], h1_l[:, i, :], i == 0, i == H1 // P - 1)
                    last.then_inc(h2_done, 1)

            def mlp3(k):
                for j in range(H2 // P):
                    pe.wait_ge(h2_ready, 2 * k + j + 1)
                    last = nc.tensor.matmul(prod_ps[0:1, 1, 0:PAIR], wt3_sb[:, j:j + 1], h2[:, j, :],
                                            start=(j == 0), stop=(j == H2 // P - 1))
                last.then_inc(y_done, 1)

            def wait_tail_copied(k, j, slot):
                if j == L2_STEP and slot == 0:
                    pe.wait_ge(out2_ready, k + 1)
                if j == L2_STEP + 1:
                    pe.wait_ge(h1_copied, 2 * k + slot + 1)
                if j == L2_STEP + 2 and slot == 0:
                    pe.wait_ge(h2_ready, 2 * k + 2)
                if j == L2_STEP + 2 and slot == 1:
                    pe.wait_ge(y_ready, k + 1)

            def step(k, j):
                s = SPP * k + j
                tile = 2 * k + j // SPT
                for c in range(CHUNKS):
                    if c == 4 and ends_tile(k, j):
                        pe.wait_ge(x3_ready, 2 * tile + 4)
                        pick_first(j + 1)
                        pick_second(j + 1, 0)
                    if c == 0 and has(s, 2):
                        multiply_layers(s - 2, j - 2, 3)
                    if c == 2:
                        if has(s, 1):
                            pe.wait_ge(x1t_ready, s)
                        else:
                            pe.wait_ge(first_ready, s + 1)
                        if ends_tile(k, j):
                            turn_parts(tile + 1, 0)
                        elif has(s + 1):
                            pick_first(j + 1)
                    if c == 3 and ends_tile(k, j):
                        pe.wait_ge(x3_ready, 2 * tile + 3)
                        turn_parts(tile + 1, 1)
                    if c == 3 and has(s, 1):
                        multiply_layers(s - 1, j - 1, 1)
                    pe.wait_ge(low_ready, entry(k, j, c) + 1)
                    if c + AHEAD < CHUNKS:
                        pick_second(j, c + AHEAD)
                    elif has(s + 1) and not (c + AHEAD == CHUNKS and ends_tile(k, j)):
                        pick_second(j + 1, c + AHEAD - CHUNKS)
                    if c == 4:
                        if has(s, 1):
                            pe.wait_ge(prod_ready, 2 * (s - 1) + 1)
                        turn_x(j)
                    layer1(k, j, c)
                    if c == 0 and has(s, 1):
                        pe.wait_ge(first_ready, s + 1)
                        turn_x1(s - 1, j - 1)
                    if (j, c) == (L2_STEP, SLOTS[0]):
                        layer2(k)
                    if (j, c) == (L2_STEP + 1, SLOTS[0]):
                        pe.wait_ge(prod_ready, 2 * (s - 1))
                        mlp1(k, 0)
                    if (j, c) == (L2_STEP + 2, SLOTS[0]):
                        pe.wait_ge(prod_ready, 2 * (s - 1))
                        mlp2(k)
                    if j > L2_STEP and c == SLOTS[1]:
                        pe.wait_ge(xb_ready, s + 1)
                        if j == L2_STEP + 1:
                            mlp1(k, 1)
                        else:
                            mlp3(k)
                    if c == 2 and has(s, 1):
                        wait_tail_copied(k, j, 0)
                        multiply_layers(s - 1, j - 1, 0)
                    if c == 6 and has(s, 1):
                        pe.wait_ge(xb_ready, s + 1)
                        wait_tail_copied(k, j, 1)
                        multiply_layers(s - 1, j - 1, 2)

            def keep_busy(n):
                for i in range(n):
                    nc.tensor.matmul(x1_ps[:, :], select[0:PARTS, 0, :],
                                     select[0:PARTS, 0:4, :].rearrange("p c r -> p (c r)"), start=True, stop=True)

            pe.wait_ge(consts_ready, 1)
            pe.wait_ge(gathered[0], 16 * NF)
            keep_busy(8)
            turn_parts(0, 0)
            keep_busy(3)
            pe.wait_ge(x3_ready, 1)
            turn_parts(0, 1)
            keep_busy(5)
            pe.wait_ge(x3_ready, 2)
            pick_first(0)
            for c in range(AHEAD):
                pick_second(0, c)
            keep_busy(6)
            pe.wait_ge(weights_ready, 4)
            for j in range(HEAD):
                step(0, j)
            pe.wait_ge(late_loaded, 16 * LATE)
            with pe.Fori(0, PAIRS - 1) as k:
                for j in range(HEAD, HEAD + SPP):
                    step(k, j)
            for j in range(HEAD, SPP):
                step(PAIRS - 1, j)
            end = STEPS - 1
            multiply_layers(end - 1, SPP - 2, 3)
            turn_x1(end, SPP - 1)
            keep_busy(2)
            multiply_layers(end, SPP - 1, 0)
            multiply_layers(end, SPP - 1, 1)
            multiply_layers(end, SPP - 1, 2, z_ps)
            multiply_layers(end, SPP - 1, 3, z_ps)
            keep_busy(12)
            layer2(PAIRS - 1)
            mlp1(PAIRS - 1, 0)
            mlp1(PAIRS - 1, 1)
            mlp2(PAIRS - 1)
            mlp3(PAIRS - 1)

        @block.scalar
        def _(act):
            def copy_hi(t, parity, k):
                act.wait_ge(gathered[parity], 16 * NF * (k + 1))
                if has(t, 1):
                    act.wait_ge(parts_turned, 2 * t)
                nc.scalar.copy(parts[:, :, 0, :], emb[:, parity, :, :].rearrange("p m d -> p d m")
                               ).then_inc(hi_ready, 1)

            def copy_mid(t):
                act.wait_ge(rest_ready, t + 1)
                nc.scalar.copy(parts[:, :, 1, :], rest[:, :, :].rearrange("p m d -> p d m")
                               ).then_inc(mid_ready, 1)

            def copy_parts(t, parity, half):
                act.wait_ge(parts_turned, 2 * t + half + 1)
                nc.scalar.copy(x3[0:PARTS, parity, :, 8 * half:8 * half + 8].rearrange("p b d -> p d b"),
                               work_ps[0:PARTS, :].bitcast(BF16).rearrange("p (d b) -> p d b", d=8)
                               ).then_inc(x3_ready, 1)

            def copy_first(s, j):
                act.wait_ge(first_picked, s + 1)
                nc.scalar.copy(first[:, j % 2, :], work_ps[:, :]).then_inc(first_ready, 1)

            def round_high(k, j, c):
                m, n, rows = SPP * CHUNKS * k + CHUNKS * j + c, entry(k, j, c), slice(0, KROWS[c])
                act.wait_ge(z_made, m + 1)
                if not isinstance(n, int) or n >= RING:
                    act.wait_ge(entry_used, n - RING + 1)
                slot = (CHUNKS * j + c) % RING
                nc.scalar.copy(ring_h[rows, slot, :], z_ps[slot][rows, :]).then_inc(high_ready, 1)

            def round_slice(k, q):
                n, fields = slice_entry(k, q), min(2, NF - 2 * q)
                act.wait_ge(entry_used, n - RING + 1)
                nc.scalar.copy(ring_h[:, slice_slot(k, q), 0:fields * PAIR],
                               prod[:, 2 * q:2 * q + fields, :].rearrange("p m b -> p (m b)")
                               ).then_inc(high_ready, 1)

            def copy_x1(s, k, j):
                act.wait_ge(entry_used, entry(k, j, CHUNKS - 1) + 1)
                nc.scalar.copy(x1[:, j % 2, :], x1_ps[:, :]).then_inc(x1_ready, 1)

            def copy_x1t(s, j):
                act.wait_ge(x1_turned, s + 1)
                nc.scalar.copy(x1t[:, j % 2, :, :].rearrange("p g n -> p (g n)"),
                               work_ps[:, :]).then_inc(x1t_ready, 1)

            def spread_x(s, j):
                act.wait_ge(x_turned, s + 1)
                for b in range(OWNERS):
                    last = nc.scalar.activation(xb[:, j % 2, :, b, 0:NF],
                                                x_ps.rearrange("p (g m) -> p g m", g=GROUPS),
                                                ACT.Copy, scale=own[:, b:b + 1])
                last.then_inc(xb_ready, 1)

            def copy_prod(s, j, half):
                act.wait_ge(prod_done, 2 * s + half + 1)
                b = (j % SPP) * STEP + half * (STEP // 2)
                nc.scalar.copy(prod[:, :, b:b + STEP // 2].rearrange("p m (q b) -> p q b m", q=STRIPS),
                               prod_ps[:, :, 0:2 * OWNERS * NM].rearrange("p q (b m) -> p q b m", m=NM)
                               ).then_inc(prod_ready, 1)

            def round_out1(k):
                nc.scalar.copy(outs_h[:, 0, :], prod[:, NF, :]).then_inc(out1_high, 1)

            def round_dense(k):
                act.wait_ge(dense_loaded, 16 * k + 16)
                nc.scalar.copy(dense_s[0:STACKED, :], dense_sb[0:STACKED, :]).then_inc(dense_high, 1)

            def round_out2(k):
                act.wait_ge(entry_used, slice_entry(k, SLICES - 1) + 1)
                nc.scalar.copy(outs_h[:, 1, :], prod_ps[:, 0, 0:PAIR]).then_inc(out2_high, 1)

            def relu1(k, half):
                act.wait_ge(h1_done, 2 * k + half + 1)
                for i in range(2):
                    last = nc.scalar.activation(h1[:, 2 * half + i, :], prod_ps[:, 1 - half, i * PAIR:(i + 1) * PAIR],
                                                ACT.Relu, bias=b1_sb[:, 2 * half + i:2 * half + i + 1])
                last.then_inc(h1_copied, 1)
                act.wait_ge(h1_copied, 2 * k + half + 1)
                nc.scalar.copy(h1_h[:, 2 * half:2 * half + 2, :], h1[:, 2 * half:2 * half + 2, :]).then_inc(h1_high, 1)

            def relu2(k):
                for i in range(H2 // P):
                    act.wait_ge(h2_done, 2 * k + i + 1)
                    nc.scalar.activation(h2[:, i, :], prod_ps[:, 1 - i, 0:PAIR],
                                         ACT.Relu, bias=b2_sb[:, i:i + 1]).then_inc(h2_ready, 1)

            def copy_y(k):
                act.wait_ge(y_done, k + 1)
                act.wait_ge(y_free, 16 * k + 16)
                nc.scalar.copy(y[0:1, :], prod_ps[0:1, 1, 0:PAIR]).then_inc(y_ready, 1)

            def step(k, j):
                s = SPP * k + j
                tile = 2 * k + j // SPT
                nxt = j // SPT + 1
                for c in range(CHUNKS):
                    if c == 6 and ends_tile(k, j):
                        copy_first(s + 1, j + 1)
                    round_high(k, j, c)
                    if c == begin_tile(j) and ends_tile(k, j):
                        copy_hi(tile + 1, nxt % 2, k + nxt // 2)
                    if c == 1 and j == L2_STEP + 2:
                        relu1(k, 1)
                    if c == 1 and has(s, 1):
                        copy_x1(s - 1, k, j - 1)
                    if c == begin_tile(j) + 1 and ends_tile(k, j):
                        copy_mid(tile + 1)
                    if c == (1 if j == L2_STEP else 2) and has(s, 2):
                        copy_prod(s - 2, j - 2, 1)
                    if (j, c) == (L2_STEP, SLOTS[0]):
                        act.wait_ge(prod_ready, 2 * (SPP * k + SPP))
                        for q in range(SLICES):
                            round_slice(k, q)
                            if q == 1:
                                copy_x1t(s - 1, j - 1)
                            if q == SLICES - 2:
                                round_out1(k)
                    if (j, c) == (L2_STEP, SLOTS[0] + 1):
                        round_out2(k)
                    if (j, c) == (L2_STEP, CHUNKS - 1):
                        round_dense(k)
                    if c == 2 and has(s, 1) and j != L2_STEP:
                        copy_x1t(s - 1, j - 1)
                    if (j, c) == (L2_STEP + 1, SLOTS[0] + 3):
                        relu1(k, 0)
                    if (j, c) == (L2_STEP + 2, SLOTS[0] + 3):
                        relu2(k)
                    if c == 4 and ends_tile(k, j):
                        copy_parts(tile + 1, nxt % 2, 0)
                    if c == 5 and ends_tile(k, j):
                        copy_parts(tile + 1, nxt % 2, 1)
                    if c == 4 and has(s + 1) and not ends_tile(k, j):
                        copy_first(s + 1, j + 1)
                    if c == 5 and has(s, 1):
                        copy_prod(s - 1, j - 1, 0)
                    if c == 6:
                        spread_x(s, j)
                    if (j, c) == (L2_STEP + 2, CHUNKS - 1):
                        copy_y(k)

            act.wait_ge(ws_summed, 1)
            nc.scalar.copy(ws_h[:, :, :], ws_a[:, :, :]).then_inc(weights_high, 1)
            act.wait_ge(weights_loaded, 16 * WEIGHT_LOADS)
            nc.scalar.copy(weights_h[:, :], stage).then_inc(weights_high, 1)
            copy_hi(0, 0, 0)
            copy_mid(0)
            copy_parts(0, 0, 0)
            copy_parts(0, 0, 1)
            copy_first(0, 0)
            for j in range(HEAD):
                step(0, j)
            with act.Fori(0, PAIRS - 1) as k:
                for j in range(HEAD, HEAD + SPP):
                    step(k, j)
            for j in range(HEAD, SPP):
                step(PAIRS - 1, j)
            end = STEPS - 1
            copy_x1(end, PAIRS - 1, SPP - 1)
            copy_prod(end - 1, SPP - 2, 1)
            copy_x1t(end, SPP - 1)
            copy_prod(end, SPP - 1, 0)
            act.wait_ge(prod_ready, 2 * STEPS)
            for q in range(SLICES):
                round_slice(PAIRS - 1, q)
                if q == SLICES - 2:
                    round_out1(PAIRS - 1)
                    round_dense(PAIRS - 1)
            round_out2(PAIRS - 1)
            relu1(PAIRS - 1, 0)
            relu1(PAIRS - 1, 1)
            relu2(PAIRS - 1)
            copy_y(PAIRS - 1)

        @block.vector
        def _(dve):
            def split_rest(t, parity):
                dve.wait_ge(hi_ready, t + 1)
                nc.vector.tensor_tensor(rest[:, :, :].rearrange("p m d -> p d m"),
                                        emb[:, parity, :, :].rearrange("p m d -> p d m"),
                                        parts[:, :, 0, :], ALU.subtract).then_inc(rest_ready, 1)

            def split_lo(t):
                dve.wait_ge(mid_ready, t + 1)
                nc.vector.tensor_tensor(parts[:, :, 2, :], rest[:, :, :].rearrange("p m d -> p d m"),
                                        parts[:, :, 1, :], ALU.subtract).then_inc(parts_ready, 1)

            def multiply_fields(k, j, c):
                dve.wait_ge(second_picked, SPP * CHUNKS * k + CHUNKS * j + c + 1)
                if c == 0:
                    dve.wait_ge(first_ready, SPP * k + j + 1)
                bank_ps = z_ps[(CHUNKS * j + c) % RING][0:KROWS[c], :]
                nc.vector.tensor_tensor(bank_ps, bank_ps, first[0:KROWS[c], j % 2, :],
                                        ALU.mult).then_inc(z_made, 1)

            def take_low(k, j, c):
                slot, rows = (CHUNKS * j + c) % RING, slice(0, KROWS[c])
                dve.wait_ge(high_ready, entry(k, j, c) + 1)
                out = ring_l[:, slot, :]
                if c == FULL:
                    rows = slice(32, 64)
                    out = ring_h[rows, slot, :]
                nc.vector.tensor_tensor(out, z_ps[slot][rows, :], ring_h[rows, slot, :],
                                        ALU.subtract).then_inc(low_ready, 1)

            def slices(k):
                for q in range(SLICES):
                    if q == SLICES - 1:
                        dve.wait_ge(out1_high, k + 1)
                        nc.vector.tensor_tensor(outs_l[:, 0, :], prod[:, NF, :], outs_h[:, 0, :],
                                                ALU.subtract).then_inc(out1_ready, 1)
                    n, slot, fields = slice_entry(k, q), slice_slot(k, q), min(2, NF - 2 * q)
                    dve.wait_ge(high_ready, n + 1)
                    nc.vector.tensor_tensor(ring_l[:, slot, 0:fields * PAIR],
                                            prod[:, 2 * q:2 * q + fields, :].rearrange("p m b -> p (m b)"),
                                            ring_h[:, slot, 0:fields * PAIR],
                                            ALU.subtract).then_inc(low_ready, 1)

            def low_out2(k):
                dve.wait_ge(out2_high, k + 1)
                nc.vector.tensor_tensor(outs_l[:, 1, :], prod_ps[:, 0, 0:PAIR], outs_h[:, 1, :],
                                        ALU.subtract).then_inc(out2_ready, 1)

            def low_dense(k):
                dve.wait_ge(dense_high, k + 1)
                nc.vector.tensor_tensor(dense_s[32:64, :], dense_sb[32:64, :], dense_s[32:64, :],
                                        ALU.subtract).then_inc(dense_ready, 1)

            def low_h1(k, half):
                dve.wait_ge(h1_high, 2 * k + half + 1)
                blocks = slice(2 * half, 2 * half + 2)
                nc.vector.tensor_tensor(h1_l[:, blocks, :], h1[:, blocks, :], h1_h[:, blocks, :],
                                        ALU.subtract).then_inc(h1_ready, 1)

            def step(k, j):
                s = SPP * k + j
                tile = 2 * k + j // SPT
                nxt = j // SPT + 1
                for c in range(CHUNKS):
                    multiply_fields(k, j, c)
                    late = (k, j, c - 1) if c else (k, j - 1, CHUNKS - 1)
                    if late[1:] == (L2_STEP, SLOTS[0] + 1):
                        slices(k)
                    if c or has(s, 1):
                        take_low(*late)
                    if (j, c) == (L2_STEP, SLOTS[0] + 2):
                        low_out2(k)
                    if (j, c) == (L2_STEP + 1, 0):
                        low_dense(k)
                    if (j, c) == (L2_STEP + 1, SLOTS[0] + 4):
                        low_h1(k, 0)
                    if (j, c) == (L2_STEP + 2, 2):
                        low_h1(k, 1)
                    if c == begin_tile(j) + 1 and ends_tile(k, j):
                        split_rest(tile + 1, nxt % 2)
                    if c == begin_tile(j) + 2 and ends_tile(k, j):
                        split_lo(tile + 1)

            nc.vector.memset(y[0:1, :], 0.0).then_inc(y_free, 16)
            dve.wait_ge(ws_loaded, 32)
            nc.vector.tensor_tensor(ws_a[:, :, :], ws_a[:, :, :], ws_b[:, :, :],
                                    ALU.add).then_inc(ws_summed, 1)
            dve.wait_ge(weights_high, 1)
            nc.vector.tensor_tensor(ws_l[:, :, :], ws_a[:, :, :], ws_h[:, :, :],
                                    ALU.subtract).then_inc(weights_ready, 1)
            dve.wait_ge(weights_ready, 1)
            nc.vector.tensor_copy(ws_h[64:96, FULL, :], ws_l[64:96, FULL, :]).then_inc(weights_ready, 1)
            dve.wait_ge(consts_loaded, 16 * CONSTS)
            nc.vector.tensor_copy(eye_bf[:, :], eye[:, :])
            nc.vector.tensor_copy(stack[0:PARTS, :], stack_f[0:PARTS, :])
            nc.vector.tensor_copy(select[0:PARTS, :, :], select_f[0:PARTS, :, :])
            for i in range(2):
                for g in range(GROUPS):
                    last = nc.vector.tensor_copy(xb[:, i, g, :, NF], own[:, :])
            last.then_inc(consts_ready, 1)
            dve.wait_ge(weights_high, 2)
            nc.vector.tensor_tensor(weights_l[:, :], stage, weights_h[:, :], ALU.subtract).then_inc(weights_ready, 1)
            dve.wait_ge(weights_ready, 3)
            nc.vector.tensor_copy(weights_h[64:STACKED, WTD_AT:WEIGHTS],
                                  weights_l[64:STACKED, WTD_AT:WEIGHTS]).then_inc(weights_ready, 1)
            split_rest(0, 0)
            split_lo(0)
            for j in range(HEAD):
                step(0, j)
            with dve.Fori(0, PAIRS - 1) as k:
                for j in range(HEAD, HEAD + SPP):
                    step(k, j)
            for j in range(HEAD, SPP):
                step(PAIRS - 1, j)
            take_low(PAIRS - 1, SPP - 1, CHUNKS - 1)
            dve.wait_ge(prod_done, 2 * STEPS)
            for q in range(STRIPS):
                b = PAIR - STEP // 2 + q * 2 * OWNERS
                last = nc.vector.tensor_copy(
                    prod[:, :, b:b + 2 * OWNERS].rearrange("p m b -> p b m"),
                    z_ps[q][:, 0:2 * OWNERS * NM].rearrange("p (b m) -> p b m", m=NM))
            last.then_inc(prod_ready, 1)
            slices(PAIRS - 1)
            low_dense(PAIRS - 1)
            low_out2(PAIRS - 1)
            low_h1(PAIRS - 1, 0)
            low_h1(PAIRS - 1, 1)


def kernel(**inputs):
    import concourse.bacc as bacc
    from concourse.bass_utils import run_bass_kernel_spmd

    nc = bacc.Bacc("TRN2", target_bir_lowering=False, num_devices=1)
    arrays = {}

    def given(name, a):
        name = "in_" + name
        arrays[name] = np.ascontiguousarray(a)
        return nc.dram_tensor(name, arrays[name].shape, mybir.dt.from_np(arrays[name].dtype),
                              kind="ExternalInput").ap()

    ids = np.asarray(inputs["ids"]).reshape(TILES, P // 16, STRIPS, 2, OWNERS, NF)
    ids = ids.transpose(1, 3, 2, 4, 0, 5).reshape(P, TILES * NF)

    w0 = np.asarray(inputs["L0_rec_W0"]).reshape(NF, NF, NO)
    w0a = np.zeros((P, CHUNKS, NO), np.float32)
    w0b = np.zeros((P, CHUNKS, NO), np.float32)
    for row, c, m, p in pair_rows()[1]:
        w0a[row, c] = w0[m, p]
        if p != m:
            w0b[row, c] = w0[p, m]

    def stacked(rows, height):
        out = np.zeros((height, rows.shape[1]), rows.dtype)
        for at in (0, 32, 64):
            out[at:at + ND] = rows
        return out

    wt1 = np.asarray(inputs["W_top1"])
    select, stack, own, eye = constants()
    args = [given("ids", ids), [given(f"tbl_{f}", inputs[f"tbl_{f}"]) for f in range(NF)],
            given("dense", stacked(np.asarray(inputs["dense_ctx"]).T, STACKED)),
            given("w0a", w0a), given("w0b", w0b), given("w1", inputs["L0_rec_W1"]),
            given("wt1", wt1[:2 * NO]), given("wt1d", stacked(wt1[2 * NO:], P)), given("wt2", inputs["W_top2"]),
            given("wt3", np.asarray(inputs["W_top3"]).reshape(H2 // P, P).T),
            given("b1", np.asarray(inputs["b_top1"]).reshape(H1 // P, P).T),
            given("b2", np.asarray(inputs["b_top2"]).reshape(H2 // P, P).T),
            given("select", select), given("stack", stack), given("own", own), given("eye", eye)]
    out = nc.dram_tensor("out_y", (BATCH, 1), F32, kind="ExternalOutput").ap()
    build(nc, *args, out)
    r = run_bass_kernel_spmd(nc, [arrays], core_ids=[0])
    return r.results[0]["out_y"]
```
